# Optimizing a Trainium2 kernel written in Bass

```python
import numpy as np
import jax
import jax.numpy as jnp

def _softmax(x, axis=-1):
    return jax.nn.softmax(x, axis=axis)

def _gelu(x):
    return jax.nn.gelu(x, approximate=True)

def _silu(x):
    return jax.nn.silu(x)

def _sigmoid(x):
    return jax.nn.sigmoid(x)

def _layernorm(x, axis=-1, eps=1e-05):
    m = jnp.mean(x, axis=axis, keepdims=True)
    v = jnp.var(x, axis=axis, keepdims=True)
    return (x - m) / jnp.sqrt(v + eps)

def _scatter_add(tgt, idx, src, axis=0):
    return tgt.at[idx].add(src)

def _segment_sum(src, seg, n):
    return jax.ops.segment_sum(src, seg, n)
kernel_name = 'mk_xattn_ffn_d2_seqx_r8_ddbb48'

def setup_inputs(seed: int=0):
    np.random.seed(seed)
    _w = jnp.asarray

    def _rec_inputs():
        import jax
        import jax.numpy as jnp
        _rk = jax.random.key(seed)
        x = -0.000125 + 0.9999 * jax.random.normal(jax.random.fold_in(_rk, 1), (4, 256, 256), jnp.float32)
        _lenS = 256 - jax.random.randint(jax.random.fold_in(_rk, 7), (4,), 0, max(1, 256 // 4) + 1, jnp.int32)
        _lenS2 = 256 - jax.random.randint(jax.random.fold_in(_rk, 8), (4,), 0, max(1, 256 // 4) + 1, jnp.int32)
        itok_BxS_13_99985 = jax.random.randint(jax.random.fold_in(_rk, 11), (4, 256), 13, 99986, jnp.int32)
        _ctx_2048P = jax.random.normal(jax.random.fold_in(_rk, 12), (4, 16, 256), jnp.float32)
        _ctx_2048c = jax.random.dirichlet(jax.random.fold_in(_rk, 512), 0.3 * jnp.ones((16,), jnp.float32), (4, 256))
        _ctx_2048t = jnp.einsum('bsk,bkd->bsd', _ctx_2048c, _ctx_2048P)
        _ctx_2048t = _ctx_2048t * jax.lax.rsqrt(jnp.mean(jnp.square(_ctx_2048t)) + 1e-12) * 0.953939
        ctx_2048 = 6.82029e-06 + 0.0200006 * (_ctx_2048t + 0.3 * jax.random.normal(jax.random.fold_in(_rk, 612), (4, 256, 256), jnp.float32))
        _validS = jnp.arange(256)[None, :] < _lenS[:, None]
        _validS2 = jnp.arange(256)[None, :] < _lenS2[:, None]
        _causal = jnp.tril(jnp.ones((256, 256), dtype=bool))
        mask_1xSxS2_ff0 = jnp.where(jnp.ones((1, 256, 256), dtype=bool), 0.0, -1000000000.0).astype(jnp.float32)
        return (x, itok_BxS_13_99985, ctx_2048, mask_1xSxS2_ff0)
    x, itok_BxS_13_99985, ctx_2048, mask_1xSxS2_ff0 = _rec_inputs()

    def _L0_xattn_setup():
        import jax, jax.numpy as jnp
        import numpy as np
        B, S, D = (4, 512, 256)
        E = 4
        F = 1024 // E
        VOCAB = 12500
        key = jax.random.key(seed)
        k1, k2, k3, k4, k5 = jax.random.split(key, 5)
        hidden_states = jax.random.normal(k1, (B, S, D), dtype=jnp.float32)
        token_ids = jax.random.randint(k2, (B, S), 0, VOCAB, dtype=jnp.int64)
        Wg = jax.random.normal(k3, (E, F, D), dtype=jnp.float32) * 0.02
        Wu = jax.random.normal(k4, (E, F, D), dtype=jnp.float32) * 0.02
        Wd = jax.random.normal(k5, (E, D, F), dtype=jnp.float32) * 0.02
        return {'hidden_states': hidden_states, 'token_ids': token_ids, 'Wg': Wg, 'Wu': Wu, 'Wd': Wd}
    _L0_xattn_all = _L0_xattn_setup()
    _L0_xattn_in = {k: v for k, v in _L0_xattn_all.items() if k in ()}
    del _L0_xattn_all

    def _L0_ffn_setup():
        import jax, jax.numpy as jnp
        import numpy as np
        EPS = 1e-05

        def _bitlinear(x, w):
            rms = jax.lax.rsqrt(jnp.maximum(jnp.mean(w * w), EPS))
            w_quant = jnp.clip(jnp.round(w * rms), -1.0, 1.0) / rms
            w_quant = jax.lax.stop_gradient(w_quant - w) + w
            scale = 127.0 / jnp.maximum(jnp.max(jnp.abs(x), axis=-1, keepdims=True), EPS)
            x_quant = jnp.clip(jnp.round(x * scale), -128.0, 127.0) / scale
            x_quant = jax.lax.stop_gradient(x_quant - x) + x
            return jnp.einsum('bsd,fd->bsf', x_quant, w_quant)
        key = jax.random.key(seed)
        k1, k2, k3 = jax.random.split(key, 3)
        n_embd, d_ff = (256, 1024)
        B, S = (4, 256)
        x = jax.random.normal(k1, (B, S, n_embd), dtype=jnp.float32)
        w1 = jax.random.normal(k2, (d_ff, n_embd), dtype=jnp.float32) * 0.02
        w2 = jax.random.normal(k3, (n_embd, d_ff), dtype=jnp.float32) * 0.02
        return {'x': x, 'w1': w1, 'w2': w2}
    _L0_ffn_all = _L0_ffn_setup()
    _L0_ffn_in = {k: v for k, v in _L0_ffn_all.items() if k in ('w1', 'w2')}
    del _L0_ffn_all

    def _L1_xattn_setup():
        import jax, jax.numpy as jnp
        import numpy as np
        H = 256
        NH = 16
        NKV = 4
        HD = 128
        GROUPS = NH // NKV
        EPS = 1e-06
        B, S, SE = (1, 256, 512)

        def _rmsnorm(x, w, eps=EPS):
            xf = x.astype(jnp.float32)
            var = jnp.mean(xf * xf, axis=-1, keepdims=True)
            return (xf * jax.lax.rsqrt(var + eps)).astype(x.dtype) * w
        key = jax.random.key(seed)
        ks = jax.random.split(key, 12)
        sc = 0.02
        return {'hidden_states': jax.random.normal(ks[0], (B, S, H), jnp.float32), 'encoder_hidden_states': jax.random.normal(ks[1], (B, SE, H), jnp.float32), 'attention_mask': jnp.zeros((B, S, SE), jnp.float32), 'Wq': jax.random.normal(ks[2], (H, NH * HD), jnp.float32) * sc, 'bq': jax.random.normal(ks[3], (NH * HD,), jnp.float32) * sc, 'Wk': jax.random.normal(ks[4], (H, NKV * HD), jnp.float32) * sc, 'bk': jax.random.normal(ks[5], (NKV * HD,), jnp.float32) * sc, 'Wv': jax.random.normal(ks[6], (H, NKV * HD), jnp.float32) * sc, 'bv': jax.random.normal(ks[7], (NKV * HD,), jnp.float32) * sc, 'Wo': jax.random.normal(ks[8], (NH * HD, H), jnp.float32) * sc, 'qn_w': jnp.ones((HD,), jnp.float32), 'kn_w': jnp.ones((HD,), jnp.float32)}
    _L1_xattn_all = _L1_xattn_setup()
    _L1_xattn_in = {k: v for k, v in _L1_xattn_all.items() if k in ('Wq', 'bq', 'Wk', 'bk', 'Wv', 'bv', 'Wo', 'qn_w', 'kn_w')}
    del _L1_xattn_all

    def _L1_ffn_setup():
        import jax, jax.numpy as jnp
        import numpy as np
        HID = 256
        N_EXP = 32
        F_EXP = 96
        TOP_K = 6
        F_SH = 192
        B, S = (1, 128)
        key = jax.random.key(seed)
        ks = jax.random.split(key, 8)
        s = 0.02
        return {'hidden_states': jax.random.normal(ks[0], (B, S, HID), dtype=jnp.float32), 'gate_w': jax.random.normal(ks[1], (HID, N_EXP), dtype=jnp.float32) * s, 'wg': jax.random.normal(ks[2], (N_EXP, HID, F_EXP), dtype=jnp.float32) * s, 'wu': jax.random.normal(ks[3], (N_EXP, HID, F_EXP), dtype=jnp.float32) * s, 'wd': jax.random.normal(ks[4], (N_EXP, F_EXP, HID), dtype=jnp.float32) * s, 'sg': jax.random.normal(ks[5], (HID, F_SH), dtype=jnp.float32) * s, 'su': jax.random.normal(ks[6], (HID, F_SH), dtype=jnp.float32) * s, 'sd': jax.random.normal(ks[7], (F_SH, HID), dtype=jnp.float32) * s}
    _L1_ffn_all = _L1_ffn_setup()
    _L1_ffn_in = {k: v for k, v in _L1_ffn_all.items() if k in ('gate_w', 'wg', 'wu', 'wd', 'sg', 'su', 'sd')}
    del _L1_ffn_all
    return {'x': x, 'itok_BxS_13_99985': itok_BxS_13_99985, 'ctx_2048': ctx_2048, 'mask_1xSxS2_ff0': mask_1xSxS2_ff0, 'L0_ffn_w1': _L0_ffn_in['w1'], 'L0_ffn_w2': _L0_ffn_in['w2'], 'L1_xattn_Wq': _L1_xattn_in['Wq'], 'L1_xattn_bq': _L1_xattn_in['bq'], 'L1_xattn_Wk': _L1_xattn_in['Wk'], 'L1_xattn_bk': _L1_xattn_in['bk'], 'L1_xattn_Wv': _L1_xattn_in['Wv'], 'L1_xattn_bv': _L1_xattn_in['bv'], 'L1_xattn_Wo': _L1_xattn_in['Wo'], 'L1_xattn_qn_w': _L1_xattn_in['qn_w'], 'L1_xattn_kn_w': _L1_xattn_in['kn_w'], 'L1_ffn_gate_w': _L1_ffn_in['gate_w'], 'L1_ffn_wg': _L1_ffn_in['wg'], 'L1_ffn_wu': _L1_ffn_in['wu'], 'L1_ffn_wd': _L1_ffn_in['wd'], 'L1_ffn_sg': _L1_ffn_in['sg'], 'L1_ffn_su': _L1_ffn_in['su'], 'L1_ffn_sd': _L1_ffn_in['sd']}

def reference(x, itok_BxS_13_99985, ctx_2048, mask_1xSxS2_ff0, L0_ffn_w1, L0_ffn_w2, L1_xattn_Wq, L1_xattn_bq, L1_xattn_Wk, L1_xattn_bk, L1_xattn_Wv, L1_xattn_bv, L1_xattn_Wo, L1_xattn_qn_w, L1_xattn_kn_w, L1_ffn_gate_w, L1_ffn_wg, L1_ffn_wu, L1_ffn_wd, L1_ffn_sg, L1_ffn_su, L1_ffn_sd):
    import jax
    import jax.numpy as jnp

    def _L0_xattn_ref(hidden_states, token_ids, Wg, Wu, Wd):
        import jax, jax.numpy as jnp
        import numpy as np
        B, S, D = (4, 512, 256)
        E = 4
        F = 1024 // E
        VOCAB = 12500
        tokens_per_expert = VOCAB // E
        tid = jnp.clip(token_ids, 0, VOCAB - 1)
        expert_ids = jnp.minimum(tid // tokens_per_expert, E - 1)
        out = jnp.zeros_like(hidden_states)
        for e in range(E):
            g = jax.nn.silu(jnp.einsum('bsd,fd->bsf', hidden_states, Wg[e]))
            u = jnp.einsum('bsd,fd->bsf', hidden_states, Wu[e])
            y = jnp.einsum('bsf,df->bsd', g * u, Wd[e])
            out = jnp.where((expert_ids == e)[..., None], y, out)
        return out

    def _L0_ffn_ref(x, w1, w2):
        import jax, jax.numpy as jnp
        import numpy as np
        EPS = 1e-05

        def _bitlinear(x, w):
            rms = jax.lax.rsqrt(jnp.maximum(jnp.mean(w * w), EPS))
            w_quant = jnp.clip(jnp.round(w * rms), -1.0, 1.0) / rms
            w_quant = jax.lax.stop_gradient(w_quant - w) + w
            scale = 127.0 / jnp.maximum(jnp.max(jnp.abs(x), axis=-1, keepdims=True), EPS)
            x_quant = jnp.clip(jnp.round(x * scale), -128.0, 127.0) / scale
            x_quant = jax.lax.stop_gradient(x_quant - x) + x
            return jnp.einsum('bsd,fd->bsf', x_quant, w_quant)
        h = _bitlinear(x, w1)
        h = jax.nn.gelu(h, approximate=False)
        out = _bitlinear(h, w2)
        return out

    def _L1_xattn_ref(hidden_states, encoder_hidden_states, attention_mask, Wq, bq, Wk, bk, Wv, bv, Wo, qn_w, kn_w):
        import jax, jax.numpy as jnp
        import numpy as np
        H = 256
        NH = 16
        NKV = 4
        HD = 128
        GROUPS = NH // NKV
        EPS = 1e-06
        B, S, SE = (1, 256, 512)

        def _rmsnorm(x, w, eps=EPS):
            xf = x.astype(jnp.float32)
            var = jnp.mean(xf * xf, axis=-1, keepdims=True)
            return (xf * jax.lax.rsqrt(var + eps)).astype(x.dtype) * w
        b, s, _ = hidden_states.shape
        se = encoder_hidden_states.shape[1]
        q = (hidden_states @ Wq + bq).reshape(b, s, NH, HD).transpose(0, 2, 1, 3)
        k = (encoder_hidden_states @ Wk + bk).reshape(b, se, NKV, HD).transpose(0, 2, 1, 3)
        v = (encoder_hidden_states @ Wv + bv).reshape(b, se, NKV, HD).transpose(0, 2, 1, 3)
        k = jnp.repeat(k, GROUPS, axis=1)
        v = jnp.repeat(v, GROUPS, axis=1)
        q = _rmsnorm(q, qn_w)
        k = _rmsnorm(k, kn_w)
        scale = 1.0 / np.sqrt(HD).astype(np.float32)
        scores = jnp.einsum('bhsd,bhed->bhse', q, k) * scale
        scores = scores + attention_mask[:, None, :, :]
        probs = jax.nn.softmax(scores.astype(jnp.float32), axis=-1).astype(q.dtype)
        out = jnp.einsum('bhse,bhed->bhsd', probs, v)
        out = out.transpose(0, 2, 1, 3).reshape(b, s, NH * HD)
        return out @ Wo

    def _L1_ffn_ref(hidden_states, gate_w, wg, wu, wd, sg, su, sd):
        import jax, jax.numpy as jnp
        import numpy as np
        HID = 256
        N_EXP = 32
        F_EXP = 96
        TOP_K = 6
        F_SH = 192
        B, S = (1, 128)
        orig_shape = hidden_states.shape
        x = hidden_states.reshape(-1, HID)
        scores = jax.nn.sigmoid(x @ gate_w)
        topk_w, topk_i = jax.lax.top_k(scores, TOP_K)
        topk_w = topk_w / (jnp.sum(topk_w, axis=-1, keepdims=True) + 1e-20)
        combine = jnp.sum(jax.nn.one_hot(topk_i, N_EXP, dtype=topk_w.dtype) * topk_w[..., None], axis=1)
        g = jnp.einsum('td,edf->tef', x, wg)
        u = jnp.einsum('td,edf->tef', x, wu)
        act = jax.nn.silu(g) * u
        routed = jnp.einsum('tef,efd,te->td', act, wd, combine)
        routed = routed.reshape(orig_shape)
        shared = jax.nn.silu(hidden_states @ sg) * (hidden_states @ su) @ sd
        return routed + shared
    x = x + _L0_xattn_ref(_layernorm(x, axis=-1), itok_BxS_13_99985, ctx_2048, ctx_2048, ctx_2048)
    x = x + _L0_ffn_ref(_layernorm(x, axis=-1), L0_ffn_w1, L0_ffn_w2)
    x = x + _L1_xattn_ref(_layernorm(x, axis=-1), ctx_2048, mask_1xSxS2_ff0, L1_xattn_Wq, L1_xattn_bq, L1_xattn_Wk, L1_xattn_bk, L1_xattn_Wv, L1_xattn_bv, L1_xattn_Wo, L1_xattn_qn_w, L1_xattn_kn_w)
    x = x + _L1_ffn_ref(_layernorm(x, axis=-1), L1_ffn_gate_w, L1_ffn_wg, L1_ffn_wu, L1_ffn_wd, L1_ffn_sg, L1_ffn_su, L1_ffn_sd)
    return x

_drawn_inputs = setup_inputs


def setup_inputs(seed=0):
    import zlib

    import numpy as np

    out = dict(_drawn_inputs(seed))
    spreads = {'L1_xattn_qn_w': (1.0, 0.6), 'L1_xattn_kn_w': (1.0, 0.6)}
    factors = {'L1_xattn_Wq': 8.0,
     'L1_xattn_bq': 8.0,
     'L1_xattn_Wk': 8.0,
     'L1_xattn_bk': 8.0,
     'L1_xattn_Wv': 8.0,
     'L1_xattn_bv': 3.267,
     'L1_xattn_Wo': 3.217,
     'L1_ffn_gate_w': 8.0,
     'L1_ffn_wg': 8.0,
     'L1_ffn_wu': 8.0,
     'L1_ffn_wd': 8.0,
     'L1_ffn_sg': 3.94,
     'L1_ffn_su': 3.873,
     'L1_ffn_sd': 3.877}
    for name, (base, spread) in spreads.items():
        noise = np.random.default_rng([zlib.crc32(name.encode()), seed]).standard_normal(out[name].shape)
        drawn = base * np.exp(spread * noise) if base else spread * noise
        out[name] = jnp.asarray(drawn.astype(out[name].dtype))
    for name, factor in factors.items():
        out[name] = (out[name] * factor).astype(out[name].dtype)
    return out
```

```python
from contextlib import ExitStack

import concourse.bass as bass
from concourse import mybir

F32 = mybir.dt.float32
F32R = mybir.dt.float32r
BF16 = mybir.dt.bfloat16
I32 = mybir.dt.int32
ALU = mybir.AluOpType
ACT = mybir.ActivationFunctionType
AX = mybir.AxisListType

P = 128
MAGIC = 12582912.0


def build_program(nc, x, itok, ctx_in, mask_in, w1, w2, Wq, bq, Wk, bk, Wv, bv, Wo, qn_w, kn_w,
                  gate_w, wg, wu, wd, sg, su, sd, out):
    B, S, D = x.shape
    T = B * S
    NT = T // P
    ND = D // P
    NE0 = ctx_in.shape[0]
    SPAN = 12500 // NE0
    FF = w1.shape[0]
    NF = FF // P
    HD = qn_w.shape[0]
    NKV = Wk.shape[1] // HD
    NH = Wq.shape[1] // HD
    G = NH // NKV
    NE, _, FE = wg.shape
    FS = sg.shape[1]
    TOPK = 6
    HALF = T // 2
    NHALF = 2
    LN_EPS, Q_EPS, RMS_EPS = 1e-5, 1e-5, 1e-6

    with ExitStack() as ctx:
        stacks = [ctx]

        def sb(name, shape, dt=F32):
            return stacks[-1].enter_context(nc.sbuf_tensor(name, shape, dt))

        def sem(name):
            return ctx.enter_context(nc.semaphore(name))

        x_sb = sb("x_sb", [P, NT, D])
        xn = sb("xn", [P, NT, D])
        xT_h = sb("xT_h", [P, ND, T], F32R)
        xT_l = sb("xT_l", [P, ND, T], F32R)
        ctxT_h = sb("ctxT_h", [P, ND, T], F32R)
        ctxT_l = sb("ctxT_l", [P, ND, T], F32R)
        ident = sb("ident", [P, P])
        identb = sb("identb", [P, P], BF16)
        ones = sb("ones", [P, P])
        neg_half = sb("neg_half", [P, NT])
        pos_half = sb("pos_half", [P, 2])
        stat6 = sb("stat6", [P, NT, 6])
        mv = sb("mv", [P, NT, 2])
        veps = sb("veps", [P, NT])
        rstd = sb("rstd", [P, NT])
        mask_sb = sb("mask_sb", [P, S // P, S])
        smalls = sb("smalls", [NH + 2, HD])
        bqT = sb("bqT", [P, NH])
        bkv = sb("bkv", [P, 2, NKV * HD])
        knq = sb("knq", [P, HD])
        gw_r = sb("gw_r", [P, ND, NE])
        gw_h = sb("gw_h", [P, ND, NE], F32R)
        gw_l = sb("gw_l", [P, ND, NE], F32R)

        ps = ctx.enter_context(nc.psum_tensor("ps", [P, 8, 512], F32))
        psb = ps[:, :, :].rearrange("p a b -> p (a b)").bitcast(BF16).rearrange("p (a b) -> p a b", a=8)

        wq_r = sb("wq_r", [P, ND, G * HD])
        wkv_r = sb("wkv_r", [P, ND, 2 * HD])
        wo_r = sb("wo_r", [P, G, D])
        wq_h = sb("wq_h", [P, ND, G * HD], F32R)
        wq_l = sb("wq_l", [P, ND, G * HD], F32R)
        wkv_h = sb("wkv_h", [P, ND, 2 * HD], F32R)
        wkv_l = sb("wkv_l", [P, ND, 2 * HD], F32R)
        wo_h = sb("wo_h", [P, G, D], F32R)
        wo_l = sb("wo_l", [P, G, D], F32R)
        kv_sb = sb("kv_sb", [P, 2, 2 * HD])
        k_sq = sb("k_sq", [P, 2, HD])
        k_ss = sb("k_ss", [P, 2])
        k_ve = sb("k_ve", [P, 2])
        k_rs = sb("k_rs", [P, 2])
        k_n = sb("k_n", [P, 2, HD])
        qnb = k_n[:, 0, :]
        kT_h = sb("kT_h", [P, B, S], F32R)
        kT_l = sb("kT_l", [P, B, S], F32R)
        v_h = sb("v_h", [P, B, 2, HD], F32R)
        v_l = sb("v_l", [P, B, 2, HD], F32R)
        q_h = sb("q_h", [P, 2, S], F32R)
        q_l = sb("q_l", [P, 2, S], F32R)
        q_sq = sb("q_sq", [P, S])
        q_ve = sb("q_ve", [P, 2, 2])
        q_rs = sb("q_rs", [P, 2, 2])
        sc = sb("sc", [P, 4, 2, S])
        nmax = sb("nmax", [P, 2, 2])
        esum = sb("esum", [P, 2, 2])
        einv = sb("einv", [P, 2, 2])
        pT_h = sb("pT_h", [P, 2, 2, S], F32R)
        pT_l = sb("pT_l", [P, 2, 2, S], F32R)
        oT_h = sb("oT_h", [P, 2, S], F32R)
        oT_l = sb("oT_l", [P, 2, S], F32R)

        layer0 = ExitStack()
        stacks.append(layer0)
        ctx_sb = sb("ctx_sb", [P, NT, D])
        itok_sb = sb("itok_sb", [P, T], I32)
        emask = sb("emask", [P, NE0, T], BF16)
        m_s = sb("m_s", [P, 2, HALF])
        m_t = sb("m_t", [P, 2, HALF])
        m_h = sb("m_h", [P, 3, HALF], F32R)
        m_l = sb("m_l", [P, 3, HALF], F32R)
        w1_sb = sb("w1_sb", [P, NF, D])
        w2_sb = sb("w2_sb", [P, ND, FF])
        wss = sb("wss", [P, 2])
        wme = sb("wme", [P, 2])
        wrms = sb("wrms", [P, 2])
        wirms = sb("wirms", [P, 2])
        w1_q = sb("w1_q", [P, NF, D], BF16)
        w2_q = sb("w2_q", [P, ND, FF], BF16)
        w1T = sb("w1T", [P, ND, FF], BF16)
        w2T = sb("w2T", [P, NF, D], BF16)
        amax = sb("amax", [P, NT])
        arec = sb("arec", [P, NT])
        ascl = sb("ascl", [P, NT])
        adeq = sb("adeq", [P, NT])
        xq = w1_q
        xqT = sc[:, 0:2, :, :].rearrange("p a b c -> p (a b c)").bitcast(BF16).rearrange("p (d t) -> p d t", d=ND)
        h_sb = ctx_sb[:, :, :].rearrange("p a b -> p (a b)").rearrange("p (a b) -> p a b", a=2)
        h_q = m_s[:, :, :].rearrange("p a b -> p (a b)").bitcast(BF16).rearrange("p (a b) -> p a b", a=2)
        hT = m_t[:, :, :].rearrange("p a b -> p (a b)").bitcast(BF16).rearrange("p (a f t) -> p a f t", a=2, f=NF)
        hmax = sb("hmax", [P, NT])
        hrec = sb("hrec", [P, NT])
        hscl = sb("hscl", [P, NT])
        hdeq = sb("hdeq", [P, NT])
        stacks.pop()
        layer0.close()

        EG = 4
        GF = EG * FE
        JT = GF // P
        NG = NE // EG
        sel = sb("sel", [3 * NE, NE * FE], BF16)
        cT = sb("cT", [3 * NE, T], BF16)
        wg_r = sb("wg_r", [P, ND, GF])
        wu_r = sb("wu_r", [P, ND, GF])
        wd_r = sb("wd_r", [P, JT, D])
        wg_h = sb("wg_h", [P, 2, ND, GF], F32R)
        wg_l = sb("wg_l", [P, 2, ND, GF], F32R)
        wu_h = sb("wu_h", [P, 2, ND, GF], F32R)
        wu_l = sb("wu_l", [P, 2, ND, GF], F32R)
        wd_h = sb("wd_h", [P, 2, JT, D], F32R)
        wd_l = sb("wd_l", [P, 2, JT, D], F32R)
        e_s = sb("e_s", [P, 2, HALF])
        e_h, e_l = (c[:, :, :].rearrange("p a b -> p (a b)")[:, 0:3 * HALF].rearrange("p (a b) -> p a b", a=3)
                    for c in (ctxT_h, ctxT_l))
        NS = 2
        FSH = FS // NS
        sgu_r = sb("sgu_r", [P, 2, ND, FS])
        sd_r = sb("sd_r", [FSH, NS, D])
        sgu_h, sgu_l = (w[:, 1, :, :].rearrange("p a b -> p (a b)").rearrange("p (m d f) -> p m d f", m=2, d=ND)
                        for w in (wg_h, wg_l))
        sd_h, sd_l = (w[0:FSH, 1, 0:NS, :] for w in (wd_h, wd_l))
        gs = sb("gs", [P, NT, NE + 2])
        grep = sb("grep", [P, NT, NE + 2])
        gtop = sb("gtop", [P, NT, 8])
        gsum = sb("gsum", [P, NT])
        grec = sb("grec", [P, NT])
        gc = sb("gc", [P, NT, NE])
        gparts = sb("gparts", [P, NT, 3, NE], BF16)
        yT = xn[:, :, :].rearrange("p a b -> p (a b)").rearrange("p (d t) -> p d t", d=ND)

        load = {n: sem("ld_" + n) for n in ("x0", "x1", "ctx", "itok", "w1", "w2", "small", "bkv", "knq", "mask", "gate",
                                            "wq", "wkv", "wo", "moe", "shared")}
        consts_made = sem("consts_made")
        pool_step = sem("pool_step")
        dve_step = sem("dve_step")
        act_step = sem("act_step")
        stat_ready = sem("stat_ready")
        rstd_ready = sem("rstd_ready")
        xn_ready = sem("xn_ready")
        xT_ps = sem("xT_ps")
        xT_hi = sem("xT_hi")
        xT_lo = sem("xT_lo")
        ctxT_ps = sem("ctxT_ps")
        ctxT_hi = sem("ctxT_hi")
        ctxT_lo = sem("ctxT_lo")
        emask_made = sem("emask_made")
        up_done = sem("up_done")
        silu_done = sem("silu_done")
        gated = sem("gated")
        masked = sem("masked")
        m_hi = sem("m_hi")
        m_lo = sem("m_lo")
        down_done = sem("down_done")
        x1_ready = sem("x1_ready")
        wss_ready = sem("wss_ready")
        wss_ps = sem("wss_ps")
        wme_ready = sem("wme_ready")
        wrms_ready = sem("wrms_ready")
        wT_ps = sem("wT_ps")
        wT_ready = sem("wT_ready")
        xq_ready = sem("xq_ready")
        xqT_ps = sem("xqT_ps")
        xqT_ready = sem("xqT_ready")
        h_ps = sem("h_ps")
        h_ready = sem("h_ready")
        h_round = sem("h_round")
        hq_ready = sem("hq_ready")
        hT_ps = sem("hT_ps")
        hT_ready = sem("hT_ready")
        y_ps = sem("y_ps")
        x2_ready = sem("x2_ready")
        small_ps = sem("small_ps")
        small_ready = sem("small_ready")
        knq_made = sem("knq_made")

        kv_split = sem("kv_split")
        wq_split = sem("wq_split")
        wo_split = sem("wo_split")
        kv_ps = sem("kv_ps")
        kv_biased = sem("kv_biased")
        k_squared = sem("k_squared")
        k_ve_ready = sem("k_ve_ready")
        k_rs_ready = sem("k_rs_ready")
        k_normed = sem("k_normed")
        v_split = sem("v_split")
        kT_ps = sem("kT_ps")
        kT_hi = sem("kT_hi")
        kT_lo = sem("kT_lo")
        q_ps = sem("q_ps")
        q_hi = sem("q_hi")
        q_squared = sem("q_squared")
        q_lo = sem("q_lo")
        q_ss = sem("q_ss")
        q_ve_ready = sem("q_ve_ready")
        q_rs_ready = sem("q_rs_ready")
        s_ps = sem("s_ps")
        s_scaled = sem("s_scaled")
        s_max = sem("s_max")
        s_exp = sem("s_exp")
        s_inv = sem("s_inv")
        s_normed = sem("s_normed")
        pT_ps = sem("pT_ps")
        pT_hi = sem("pT_hi")
        pT_lo = sem("pT_lo")
        o_ps = sem("o_ps")
        o_hi = sem("o_hi")
        o_lo = sem("o_lo")
        y_done = sem("y_done")
        y_added = sem("y_added")
        wo_used = sem("wo_used")

        gw_split = sem("gw_split")
        shared_split = sem("shared_split")
        moe_split = sem("moe_split")
        sel_made = sem("sel_made")
        sel_copied = sem("sel_copied")
        gate_ps = sem("gate_ps")
        gate_sig = sem("gate_sig")
        parts_ready = sem("parts_ready")
        cT_ps = sem("cT_ps")
        cT_ready = sem("cT_ready")
        eg_ps = sem("eg_ps")
        eu_ps = sem("eu_ps")
        ec_ps = sem("ec_ps")
        e_silu = sem("e_silu")
        e_mult = sem("e_mult")
        e_comb = sem("e_comb")
        e_hi = sem("e_hi")
        e_lo = sem("e_lo")
        e_down = sem("e_down")
        yT_ready = sem("yT_ready")
        yb_ps = sem("yb_ps")
        out_ready = sem("out_ready")
        stored = sem("stored")

        chain = sem("pool_attention_step")
        moe_chain = sem("pool_expert_step")
        act_scale_ready = sem("act_scale_ready")
        w_round = sem("w_round")
        pool_waits = sem("pool_waits")
        act_waits = sem("act_waits")

        XT_UNITS = NHALF * ND

        def three(pe, dst, wh, wl, vh, vl, start, stop, **kw):
            pe.matmul(dst, wh, vh, start=start, stop=False, **kw)
            pe.matmul(dst, wh, vl, start=False, stop=False, **kw)
            return pe.matmul(dst, wl, vh, start=False, stop=stop, **kw)

        block = ctx.enter_context(nc.Block())

        LAG_Q, LAG_S, LAG_MAX, LAG_EXP, LAG_T, LAG_PV, LAG_WO = 1, 2, 3, 4, 5, 6, 7
        NSTEP = B * G
        FIRST = LAG_WO
        UPG = JT * NHALF
        UNITS = 2 * UPG
        LAG_DOWN = 2

        KV_LEAD = 3

        def kv_batch(k):
            return (k + KV_LEAD) // G if (k + KV_LEAD) % G == 0 else None

        @block.sync
        def _(sp):
            x_v = x.rearrange("b (t p) d -> p (b t) d", p=P)
            for n in range(NHALF):
                sp.dma_start(x_sb[:, n * NT // 2:(n + 1) * NT // 2, :],
                             x_v[:, n * NT // 2:(n + 1) * NT // 2, :]).then_inc(load[f"x{n}"], 16)
            sp.dma_start(ctx_sb[:, :, :], ctx_in.rearrange("b (t p) d -> p (b t) d", p=P)).then_inc(load["ctx"], 16)
            sp.dma_start(itok_sb[:, :], itok.rearrange("b s -> (b s)").unsqueeze(0).broadcast_to([P, T])).then_inc(load["itok"], 16)
            sp.dma_start(w1_sb[:, :, :], w1.rearrange("(t p) d -> p t d", p=P)).then_inc(load["w1"], 16)
            sp.dma_start(w2_sb[:, :, :], w2.rearrange("(t p) d -> p t d", p=P)).then_inc(load["w2"], 16)
            sp.dma_start(smalls[0:NH, :], bq.rearrange("(h d) -> h d", d=HD)).then_inc(load["small"], 16)
            sp.dma_start(smalls[NH:NH + 1, :], qn_w.unsqueeze(0)).then_inc(load["small"], 16)
            sp.dma_start(smalls[NH + 1:NH + 2, :], kn_w.unsqueeze(0)).then_inc(load["small"], 16)
            sp.dma_start(bkv[:, 0, :], bk.unsqueeze(0).broadcast_to([P, NKV * HD])).then_inc(load["bkv"], 16)
            sp.dma_start(bkv[:, 1, :], bv.unsqueeze(0).broadcast_to([P, NKV * HD])).then_inc(load["bkv"], 16)
            sp.dma_start(qnb, qn_w.unsqueeze(0).broadcast_to([P, HD])).then_inc(load["knq"], 16)
            sp.dma_start(knq[:, :], kn_w.unsqueeze(0).broadcast_to([P, HD])).then_inc(load["knq"], 16)
            sp.dma_start(mask_sb[:, :, :], mask_in[0].rearrange("(t p) k -> p t k", p=P)).then_inc(load["mask"], 16)
            sp.dma_start(gw_r[:, :, :], gate_w.rearrange("(t p) e -> p t e", p=P)).then_inc(load["gate"], 16)

            def load_heads(kv, after):
                if after:
                    sp.wait_ge(kv_split, kv)
                sp.dma_start(wkv_r[:, :, 0:HD], Wk.rearrange("(t p) n -> p t n", p=P)[:, :, bass.ds(kv * HD, HD)]).then_inc(load["wkv"], 16)
                sp.dma_start(wkv_r[:, :, HD:2 * HD], Wv.rearrange("(t p) n -> p t n", p=P)[:, :, bass.ds(kv * HD, HD)]).then_inc(load["wkv"], 16)
                if after:
                    sp.wait_ge(wq_split, kv * G)
                sp.dma_start(wq_r[:, :, :], Wq.rearrange("(t p) n -> p t n", p=P)[:, :, bass.ds(kv * G * HD, G * HD)]).then_inc(load["wq"], 16)
                if after:
                    sp.wait_ge(wo_split, kv * G)
                sp.dma_start(wo_r[:, :, :], Wo.rearrange("(h p) n -> p h n", p=P)[:, bass.ds(kv * G, G), :]).then_inc(load["wo"], 16)

            load_heads(0, False)
            sp.wait_ge(x2_ready, NT)
            sp.wait_ge(sel_made, 1)
            for part in range(1, 3):
                sp.dma_start(sel[part * NE:(part + 1) * NE, :], sel[0:NE, :]).then_inc(sel_copied, 16)
            for n, w in enumerate((sg, su)):
                sp.dma_start(sgu_r[:, n, :, :], w.rearrange("(t p) f -> p t f", p=P)).then_inc(load["shared"], 16)
            sp.dma_start(sd_r[:, :, :], sd.rearrange("(t p) d -> p t d", p=FSH)).then_inc(load["shared"], 16)

            with sp.Fori(1, NKV) as kv:
                load_heads(kv, True)

            wd_v = wd.rearrange("e f d -> (e f) d").rearrange("(j p) d -> p j d", p=P)

            def load_experts(g):
                for t in range(ND):
                    sp.dma_start(wg_r[:, t, :].rearrange("p (e f) -> p e f", f=FE),
                                 wg[bass.ds(g * EG, EG), t * P:(t + 1) * P, :].rearrange("e p f -> p e f")).then_inc(load["moe"], 16)
                    sp.dma_start(wu_r[:, t, :].rearrange("p (e f) -> p e f", f=FE),
                                 wu[bass.ds(g * EG, EG), t * P:(t + 1) * P, :].rearrange("e p f -> p e f")).then_inc(load["moe"], 16)
                sp.dma_start(wd_r[:, :, :], wd_v[:, bass.ds(g * JT, JT), :]).then_inc(load["moe"], 16)

            load_experts(0)
            with sp.Fori(1, NG) as g:
                sp.wait_ge(moe_split, g * 6)
                load_experts(g)

            out_v = out.rearrange("b (t p) d -> p (b t) d", p=P)
            for n in range(NT // 2):
                sp.wait_ge(out_ready, n + 1)
                sp.dma_start(out_v[:, 2 * n:2 * n + 2, :], x_sb[:, 2 * n:2 * n + 2, :]).then_inc(stored, 16)
            sp.wait_ge(stored, 16 * (NT // 2))

        def wait_alone(eng, semaphore, value, passed):
            eng.wait_ge(semaphore, value)
            if not isinstance(value, int):
                eng.sem_inc(passed, 1)

        def run_attention(eng, body):
            for k in range(-KV_LEAD, FIRST):
                body(0, k, False)
            with eng.Fori(0, NKV - 1) as i:
                for k in range(FIRST, FIRST + NSTEP):
                    body(i, k, False)
            for k in range(FIRST, FIRST + NSTEP):
                body(NKV - 1, k, True)

        def run_experts(eng, body):
            for k in range(LAG_DOWN):
                body(0, k, False)
            with eng.Fori(0, NG // 2 - 1) as i:
                for k in range(LAG_DOWN, LAG_DOWN + UNITS):
                    body(i, k, False)
            for k in range(LAG_DOWN, LAG_DOWN + UNITS):
                body(NG // 2 - 1, k, True)

        @block.gpsimd
        def _(pool):
            step = [0]

            def link(ins):
                step[0] += 1
                ins.then_inc(pool_step, 1)
                pool.wait_ge(pool_step, step[0])

            link(pool.memset(ident[:, :], 0.0))
            link(pool.affine_select(out=ident[:, :], in_=ident[:, :], compare_op=ALU.not_equal, fill=1.0, base=0,
                                    pattern=[[-1, P]], channel_multiplier=1))
            pool.memset(neg_half[:, :], -0.5)
            pool.memset(pos_half[:, :], 0.5)
            pool.memset(ones[:, :], 1.0)
            pool.tensor_copy(identb[:, :], ident[:, :]).then_inc(consts_made, 1)
            pool.wait_ge(consts_made, 1)

            def norm_scale(n):
                pool.wait_ge(stat_ready, n + 1)
                pool.tensor_tensor(rstd[:, :], veps[:, :], neg_half[:, :], ALU.pow).then_inc(rstd_ready, 1)

            norm_scale(0)
            pool.wait_ge(wme_ready, 1)
            pool.tensor_tensor(wrms[:, :], wme[:, :], neg_half[:, 0:2], ALU.pow)
            pool.tensor_tensor(wirms[:, :], wme[:, :], pos_half[:, :], ALU.pow).then_inc(wrms_ready, 1)
            for u in range(NE0 * ND * NHALF):
                e, n = u // (ND * NHALF), u % NHALF
                pool.wait_ge(gated, u + 1)
                if u == 0:
                    pool.wait_ge(emask_made, 1)
                pool.tensor_tensor(m_t[:, u % 2, :], m_t[:, u % 2, :], emask[:, e, n * HALF:(n + 1) * HALF],
                                   ALU.mult).then_inc(masked, 1)
            def split(h, l, r, done):
                step[0] += 1
                pool.tensor_copy(h, r).then_inc(pool_step, 1)
                pool.wait_ge(pool_step, step[0])
                pool.tensor_tensor(l, r, h.bitcast(F32), ALU.subtract).then_inc(done, 1)

            norm_scale(1)
            pool.wait_ge(load["wkv"], 32)
            split(wkv_h[:, :, :], wkv_l[:, :, :], wkv_r[:, :, :], kv_split)
            pool.wait_ge(load["wq"], 16)
            for h in range(G):
                split(wq_h[:, :, h * HD:(h + 1) * HD], wq_l[:, :, h * HD:(h + 1) * HD],
                      wq_r[:, :, h * HD:(h + 1) * HD], wq_split)
            pool.wait_ge(load["wo"], 16)
            pool.wait_ge(load["gate"], 16)
            split(gw_h[:, :, :], gw_l[:, :, :], gw_r[:, :, :], gw_split)
            pool.wait_ge(load["knq"], 32)
            pool.tensor_tensor(knq[:, :], knq[:, :], qnb, ALU.mult).then_inc(knq_made, 1)
            for t in range(NT):
                pool.wait_ge(h_round, t + 1)
                if t >= 2:
                    pool.wait_ge(hT_ps, t - 1)
                pool.tensor_scalar(h_q[:, t % 2, :], h_sb[:, t % 2, :], 1.0, -MAGIC, ALU.mult, ALU.add).then_inc(hq_ready, 1)
                if t < G:
                    split(wo_h[:, t, :], wo_l[:, t, :], wo_r[:, t, :], wo_split)
            norm_scale(2)


            pool.wait_ge(x2_ready, NT)
            s_v = sel[0:NE, :]
            link(pool.memset(s_v, 1.0))
            link(pool.affine_select(out=s_v, in_=s_v, compare_op=ALU.is_ge, fill=0.0, base=0,
                                    pattern=[[1, NE * FE]], channel_multiplier=-FE))
            pool.affine_select(out=s_v, in_=s_v, compare_op=ALU.is_ge, fill=0.0, base=FE - 1,
                               pattern=[[-1, NE * FE]], channel_multiplier=FE).then_inc(sel_made, 1)

            def split_in_loop(h, l, r, done, value):
                pool.tensor_copy(h, r).then_inc(chain, 1)
                pool.wait_ge(chain, value)
                pool.tensor_tensor(l, r, h.bitcast(F32), ALU.subtract).then_inc(done, 1)

            def attention(i, k, last):
                def live(j):
                    return j >= 0 and not (last and j >= NSTEP)

                b = kv_batch(k - 1)
                if b is not None and not (last and b >= B):
                    c = B * i + b
                    wait_alone(pool, kv_biased, c + 1, pool_waits)
                    pool.tensor_copy(v_h[:, b % B, :, :], kv_sb[:, :, HD:2 * HD]).then_inc(v_split, 1)
                    pool.wait_ge(v_split, 2 * c + 1)
                    pool.tensor_tensor(v_l[:, b % B, :, :], kv_sb[:, :, HD:2 * HD], v_h[:, b % B, :, :].bitcast(F32),
                                       ALU.subtract).then_inc(v_split, 1)
                j = k - LAG_EXP
                if live(j):
                    wait_alone(pool, s_inv, NSTEP * i + j + 1, pool_waits)
                    for t in range(2):
                        pool.tensor_scalar(sc[:, j % 4, t, :], sc[:, j % 4, t, :], einv[:, j % 2, t:t + 1], 1.0,
                                           ALU.mult, ALU.mult).then_inc(s_normed, 1)
                if b is not None and not (last and b >= B):
                    pool.wait_ge(k_ve_ready, c + 1)
                    pool.tensor_tensor(k_rs[:, :], k_ve[:, :], neg_half[:, 0:2], ALU.pow).then_inc(k_rs_ready, 1)
                j = k - LAG_Q
                if live(j):
                    pool.wait_ge(q_ve_ready, NSTEP * i + j + 1)
                    pool.tensor_tensor(q_rs[:, j % 2, :], q_ve[:, j % 2, :], neg_half[:, 0:2], ALU.pow).then_inc(q_rs_ready, 1)
                if last or k < FIRST:
                    return
                if k == G * (B - 1) - KV_LEAD + 1:
                    wait_alone(pool, load["wkv"], 32 * i + 64, pool_waits)
                    wait_alone(pool, kv_ps, B * i + B, pool_waits)
                    split_in_loop(wkv_h[:, :, :], wkv_l[:, :, :], wkv_r[:, :, :], kv_split, 9 * i + 1)
                h = k - (NSTEP - G + 1)
                if 0 <= h < G:
                    if h == 0:
                        wait_alone(pool, load["wq"], 16 * i + 32, pool_waits)
                    wait_alone(pool, q_ps, NSTEP * i + NSTEP - G + h + 1, pool_waits)
                    split_in_loop(wq_h[:, :, h * HD:(h + 1) * HD], wq_l[:, :, h * HD:(h + 1) * HD],
                                  wq_r[:, :, h * HD:(h + 1) * HD], wq_split, 9 * i + 2 + h)
                end = LAG_WO + NSTEP - 1
                hs = [k - end + 2] if end - 2 <= k < end else [2, 3] if k == end else []
                for h in hs:
                    if h == 0:
                        wait_alone(pool, load["wo"], 16 * i + 32, pool_waits)
                    wait_alone(pool, wo_used, NSTEP * i + NSTEP - G + h + 1, pool_waits)
                    split_in_loop(wo_h[:, h, :], wo_l[:, h, :], wo_r[:, h, :], wo_split, 9 * i + 6 + h)

            run_attention(pool, attention)
            norm_scale(3)
            pool.wait_ge(load["shared"], 48)
            split(sgu_h[:, 0, :, :], sgu_l[:, 0, :, :], sgu_r[:, 0, :, :], shared_split)
            split(sgu_h[:, 1, :, :], sgu_l[:, 1, :, :], sgu_r[:, 1, :, :], shared_split)
            split(sd_h[:, :, :], sd_l[:, :, :], sd_r[:, :, :], shared_split)

            def split_group(g, slot, first):
                wait_alone(pool, load["moe"], (g + 1) * 16 * (2 * ND + 1), pool_waits)
                if not first:
                    wait_alone(pool, e_down, (g - 1) * UPG + NS * NHALF, pool_waits)
                n = 0
                parts = [(wg_h, wg_l, wg_r, t) for t in range(ND)] + [(wu_h, wu_l, wu_r, t) for t in range(ND)]
                for h, l, r, t in parts:
                    n += 1
                    pool.tensor_copy(h[:, slot, t, :], r[:, t, :]).then_inc(moe_chain, 1)
                    pool.wait_ge(moe_chain, g * 6 + n)
                    pool.tensor_tensor(l[:, slot, t, :], r[:, t, :], h[:, slot, t, :].bitcast(F32), ALU.subtract).then_inc(moe_split, 1)
                for a, b in ((0, 2), (2, JT)):
                    n += 1
                    pool.tensor_copy(wd_h[:, slot, a:b, :], wd_r[:, a:b, :]).then_inc(moe_chain, 1)
                    pool.wait_ge(moe_chain, g * 6 + n)
                    pool.tensor_tensor(wd_l[:, slot, a:b, :], wd_r[:, a:b, :], wd_h[:, slot, a:b, :].bitcast(F32), ALU.subtract).then_inc(moe_split, 1)

            split_group(0, 0, True)
            split_group(1, 1, False)
            with pool.Fori(1, NG // 2) as i:
                split_group(2 * i, 0, False)
                split_group(2 * i + 1, 1, False)

        @block.tensor
        def _(pe):
            def to_feature_major(src, dst_sem, bank0, n, ready=None):
                for d in range(ND):
                    for t in range(NT // 2):
                        last = pe.transpose(ps[:, bank0 + ND * n + d, t * P:(t + 1) * P],
                                            src[:, n * NT // 2 + t, d * P:(d + 1) * P], ident[:, :])
                    last.then_inc(dst_sem, 1)

            def norm_transposes(m, bank0):
                for n in range(NHALF):
                    pe.wait_ge(xn_ready, m * NHALF + n + 1)
                    to_feature_major(xn, xT_ps, bank0, n)

            pe.wait_ge(consts_made, 1)
            pe.wait_ge(load["ctx"], 16)
            for n in range(NHALF):
                to_feature_major(ctx_sb, ctxT_ps, 4, n)
            norm_transposes(0, 0)
            pe.wait_ge(ctxT_lo, XT_UNITS)
            pe.wait_ge(xT_lo, XT_UNITS)
            pe.wait_ge(wss_ready, 2)
            pe.matmul(ps[:, 0, 0:2], ones[:, :], wss[:, :], start=True, stop=True).then_inc(wss_ps, 1)
            pe.wait_ge(load["small"], 48)
            pe.transpose(ps[:, 1, 0:NH + 2], smalls[:, :], ident[0:NH + 2, 0:NH + 2]).then_inc(small_ps, 1)
            pe.wait_ge(wme_ready, 1)
            pe.wait_ge(small_ready, 1)

            units = NE0 * ND * NHALF

            def up(u):
                e, f, n = u // (ND * NHALF), u // NHALF % ND, u % NHALF
                if u >= 4:
                    pe.wait_ge(gated, u - 3)
                col = slice(e * D + f * P, e * D + (f + 1) * P)
                for d in range(ND):
                    last = three(pe, ps[:, u % 4, :], ctxT_h[:, d, col], ctxT_l[:, d, col],
                                 xT_h[:, d, n * HALF:(n + 1) * HALF], xT_l[:, d, n * HALF:(n + 1) * HALF],
                                 d == 0, d == ND - 1)
                last.then_inc(up_done, 1)

            def down(u):
                e, f, n = u // (ND * NHALF), u // NHALF % ND, u % NHALF
                pe.wait_ge(m_lo, u + 1)
                for t in range(NT // 2):
                    tile = n * NT // 2 + t
                    last = three(pe, ps[:, 4 + tile // 2, tile % 2 * D:(tile % 2 + 1) * D],
                                 m_h[:, u % 3, t * P:(t + 1) * P], m_l[:, u % 3, t * P:(t + 1) * P],
                                 ctxT_h[:, f, e * D:(e + 1) * D], ctxT_l[:, f, e * D:(e + 1) * D],
                                 e == 0 and f == 0 and tile % 2 == 0, e == NE0 - 1 and f == ND - 1,
                                 skip_group_check=True)
                last.then_inc(down_done, 1)

            for u in range(units + 2):
                if u < units:
                    up(u)
                if u >= 2:
                    down(u - 2)

            pe.wait_ge(w_round, 6)
            for d in range(ND):
                for f in range(NF):
                    last = pe.transpose(psb[:, d, f * P:(f + 1) * P], w1_q[:, f, d * P:(d + 1) * P], identb[:, :])
                last.then_inc(wT_ps, 1)
            pe.wait_ge(w_round, 12)
            for h in range(2):
                for f in range(NF // 2):
                    for d in range(ND):
                        last = pe.transpose(psb[:, 2 + h, f * D + d * P:f * D + (d + 1) * P],
                                            w2_q[:, d, (h * NF // 2 + f) * P:(h * NF // 2 + f + 1) * P], identb[:, :])
                last.then_inc(wT_ps, 1)
            pe.wait_ge(xq_ready, 1)
            for d in range(ND):
                for t in range(NT):
                    last = pe.transpose(psb[:, 4 + d, t * P:(t + 1) * P], xq[:, t, d * P:(d + 1) * P], identb[:, :])
                last.then_inc(xqT_ps, 1)
            pe.wait_ge(xqT_ready, 2)
            pe.wait_ge(wT_ready, 4)

            def ffn_up(t):
                if t >= 2:
                    pe.wait_ge(h_ready, t - 1)
                for h in range(2):
                    for d in range(ND):
                        last = pe.matmul(ps[:, 2 * (t % 2) + h, :], xqT[:, d, t * P:(t + 1) * P],
                                         w1T[:, d, h * 512:(h + 1) * 512], start=(d == 0), stop=(d == ND - 1))
                last.then_inc(h_ps, 1)

            def ffn_transpose(t):
                pe.wait_ge(hq_ready, t + 1)
                if t >= 2:
                    pe.wait_ge(hT_ready, t - 1)
                for f in range(NF):
                    last = pe.transpose(psb[:, 4 + t % 2, f * P:(f + 1) * P], h_q[:, t % 2, f * P:(f + 1) * P], identb[:, :])
                last.then_inc(hT_ps, 1)

            def ffn_down(t):
                pe.wait_ge(hT_ready, t + 1)
                if t >= 2:
                    pe.wait_ge(x2_ready, t - 1)
                for f in range(NF):
                    last = pe.matmul(ps[:, 6 + t % 2, 0:D], hT[:, t % 2, f, :], w2T[:, f, :], start=(f == 0), stop=(f == NF - 1))
                last.then_inc(y_ps, 1)

            for t in range(NT + 2):
                if t < NT:
                    ffn_up(t)
                if 1 <= t <= NT:
                    ffn_transpose(t - 1)
                if t >= 2:
                    ffn_down(t - 2)
            norm_transposes(2 - 1, 0)
            pe.wait_ge(xT_lo, 2 * XT_UNITS)

            def attention(i, k, last_turn):
                g = NSTEP * i

                def live(j):
                    return j >= 0 and not (last_turn and j >= NSTEP)

                j = k - LAG_T
                if live(j):
                    pe.wait_ge(s_normed, 2 * (g + j) + 2)
                    if j >= 2:
                        pe.wait_ge(pT_lo, g + j - 1)
                    for kt in range(2):
                        for t in range(2):
                            last = pe.transpose(ps[:, 4 + j % 2, kt * S + t * P:kt * S + (t + 1) * P],
                                                sc[:, j % 4, t, kt * P:(kt + 1) * P], ident[:, :])
                    last.then_inc(pT_ps, 1)
                j = k - LAG_PV
                if live(j):
                    b = j // G % B
                    pe.wait_ge(pT_lo, g + j + 1)
                    if j % G == 0:
                        pe.wait_ge(v_split, 2 * (B * i + j // G + 1))
                    if j >= 1:
                        pe.wait_ge(o_lo, g + j)
                    for kt in range(2):
                        last = three(pe, ps[:, 6, 0:S], v_h[:, b, kt, :], v_l[:, b, kt, :], pT_h[:, j % 2, kt, :],
                                     pT_l[:, j % 2, kt, :], kt == 0, kt == 1)
                    last.then_inc(o_ps, 1)
                j = k - LAG_WO
                if live(j):
                    h = j % G
                    if j < G:
                        pe.wait_ge(wo_split, G * i + h + 1)
                    pe.wait_ge(o_lo, g + j + 1)
                    if h == 0:
                        pe.wait_ge(y_added, B * i + j // G + 1)
                    for t in range(2):
                        last = three(pe, ps[:, 7, t * D:(t + 1) * D], oT_h[:, j % 2, t * P:(t + 1) * P],
                                     oT_l[:, j % 2, t * P:(t + 1) * P], wo_h[:, h, :], wo_l[:, h, :],
                                     h == 0 and t == 0, h == G - 1, skip_group_check=True)
                    last.then_inc(wo_used, 1)
                j = k - LAG_Q
                if live(j):
                    pe.wait_ge(q_squared, g + j + 1)
                    pe.wait_ge(q_lo, g + j + 1)
                    for t in range(2):
                        last = pe.matmul(ps[:, 0, S + t:S + t + 1], q_sq[:, t * P:(t + 1) * P], ones[:, 0:1], start=True, stop=True)
                    last.then_inc(q_ss, 1)
                j = k - LAG_S
                if live(j):
                    if j >= 2:
                        pe.wait_ge(s_scaled, g + j - 1)
                    b = j // G % B
                    if j % G == 0:
                        pe.wait_ge(kT_lo, B * i + j // G + 1)
                    for t in range(2):
                        last = three(pe, ps[:, 2 + j % 2, t * S:(t + 1) * S], q_h[:, j % 2, t * P:(t + 1) * P],
                                     q_l[:, j % 2, t * P:(t + 1) * P], kT_h[:, b, :], kT_l[:, b, :], True, True)
                    last.then_inc(s_ps, 1)
                j = k
                if live(j):
                    b, h = j // G % B, j % G
                    if j % G == j:
                        pe.wait_ge(wq_split, G * i + h + 1)
                    elif j >= NSTEP:
                        pe.wait_ge(wq_split, G * i + G + h + 1)
                    if j >= 1:
                        pe.wait_ge(q_ve_ready, g + j)
                    for d in range(ND):
                        last = three(pe, ps[:, 0, 0:S], wq_h[:, d, h * HD:(h + 1) * HD], wq_l[:, d, h * HD:(h + 1) * HD],
                                     xT_h[:, d, b * S:(b + 1) * S], xT_l[:, d, b * S:(b + 1) * S], d == 0, d == ND - 1)
                    last.then_inc(q_ps, 1)
                b = kv_batch(k)
                if b is not None and not (last_turn and b >= B):
                    c = B * i + b
                    pe.wait_ge(kv_split, i + b // B + 1)
                    if not (k < FIRST and b == 0):
                        pe.wait_ge(kT_lo, c)
                    tok = (b % B) * S
                    for t in range(2):
                        for d in range(ND):
                            last = three(pe, ps[:, 1, t * 2 * HD:(t + 1) * 2 * HD],
                                         ctxT_h[:, d, tok + t * P:tok + (t + 1) * P], ctxT_l[:, d, tok + t * P:tok + (t + 1) * P],
                                         wkv_h[:, d, :], wkv_l[:, d, :], d == 0, d == ND - 1)
                    last.then_inc(kv_ps, 1)
                b = kv_batch(k - 2)
                if b is not None and not (last_turn and b >= B):
                    pe.wait_ge(k_normed, B * i + b + 1)
                    for t in range(2):
                        last = pe.transpose(ps[:, 1, t * P:(t + 1) * P], k_n[:, t, :], ident[:, :])
                    last.then_inc(kT_ps, 1)

            run_attention(pe, attention)

            norm_transposes(2, 0)
            pe.wait_ge(xT_lo, 3 * XT_UNITS)
            pe.wait_ge(gw_split, 1)
            for t in range(NT):
                for d in range(ND):
                    last = three(pe, ps[:, 0, t * NE:(t + 1) * NE], xT_h[:, d, t * P:(t + 1) * P], xT_l[:, d, t * P:(t + 1) * P],
                                 gw_h[:, d, :], gw_l[:, d, :], d == 0, d == ND - 1)
            last.then_inc(gate_ps, 1)
            pe.wait_ge(gate_sig, 1)

            def shared_up(u):
                f, n = u // NHALF, u % NHALF
                tok = slice(n * HALF, (n + 1) * HALF)
                if u >= 2:
                    pe.wait_ge(e_comb, u - 1)
                for m, done in ((0, eg_ps), (1, eu_ps)):
                    for d in range(ND):
                        last = three(pe, ps[0:FSH, 2 * (u % 2) + m, :], sgu_h[:, m, d, f * FSH:(f + 1) * FSH],
                                     sgu_l[:, m, d, f * FSH:(f + 1) * FSH], xT_h[:, d, tok], xT_l[:, d, tok], d == 0, d == ND - 1)
                    last.then_inc(done, 1)

            def shared_down(u):
                f, n = u // NHALF, u % NHALF
                pe.wait_ge(e_lo, u + 1)
                for d in range(ND):
                    last = three(pe, ps[:, 4 + ND * n + d, :], sd_h[:, f, d * P:(d + 1) * P], sd_l[:, f, d * P:(d + 1) * P],
                                 e_h[0:FSH, u % 3, :], e_l[0:FSH, u % 3, :], f == 0, False, skip_group_check=True)
                last.then_inc(e_down, 1)

            pe.wait_ge(shared_split, 3)
            SU = NS * NHALF
            for u in range(SU + 2):
                if u < SU:
                    shared_up(u)
                if u >= 2:
                    shared_down(u - 2)
            pe.wait_ge(parts_ready, 1)
            pe.wait_ge(e_comb, SU)
            for t in range(NT):
                last = pe.transpose(psb[0:3 * NE, 0, t * P:(t + 1) * P],
                                    gparts[:, t, :, :].rearrange("p a e -> p (a e)"), identb[:, :])
            last.then_inc(cT_ps, 1)
            pe.wait_ge(cT_ready, 1)
            pe.wait_ge(sel_copied, 32)

            def experts(i, k, last_turn):
                u0 = UNITS * i + SU
                if not (last_turn and k >= UNITS):
                    slot, f, n = k // UPG % 2, k % UPG // NHALF, k % NHALF
                    tok = slice(n * HALF, (n + 1) * HALF)
                    if k % UPG == 0:
                        pe.wait_ge(moe_split, 6 * (2 * i + k // UPG + 1))
                    pe.wait_ge(e_comb, u0 + k - 1)
                    for m, wh, wl, done in ((0, wg_h, wg_l, eg_ps), (1, wu_h, wu_l, eu_ps)):
                        for d in range(ND):
                            last = three(pe, ps[:, 2 * (k % 2) + m, :], wh[:, slot, d, f * P:(f + 1) * P],
                                         wl[:, slot, d, f * P:(f + 1) * P], xT_h[:, d, tok], xT_l[:, d, tok],
                                         d == 0, d == ND - 1)
                        last.then_inc(done, 1)
                    pe.wait_ge(e_silu, u0 + k + 1)
                    col = (2 * i + k // UPG) * GF + f * P
                    pe.matmul(ps[:, 2 * (k % 2), :], sel[:, bass.ds(col, P)], cT[:, tok], start=True, stop=True).then_inc(ec_ps, 1)
                j = k - LAG_DOWN
                if j >= 0:
                    slot, f, n = j // UPG % 2, j % UPG // NHALF, j % NHALF
                    pe.wait_ge(e_lo, u0 + j + 1)
                    for d in range(ND):
                        last = three(pe, ps[:, 4 + ND * n + d, :], wd_h[:, slot, f, d * P:(d + 1) * P],
                                     wd_l[:, slot, f, d * P:(d + 1) * P], e_h[:, j % 3, :], e_l[:, j % 3, :],
                                     False, last_turn and j >= UNITS - NHALF, skip_group_check=True)
                    last.then_inc(e_down, 1)

            run_experts(pe, experts)

            for n in range(NT // 2):
                pe.wait_ge(yT_ready, ND * (n // 2 + 1))
                for t in range(2):
                    for d in range(ND):
                        last = pe.transpose(ps[:, n, t * D + d * P:t * D + (d + 1) * P],
                                            yT[:, d, (2 * n + t) * P:(2 * n + t + 1) * P], ident[:, :])
                last.then_inc(yb_ps, 1)

        @block.scalar
        def _(act):
            act.wait_ge(consts_made, 1)

            def norm_high(m, bank0):
                for c in range(XT_UNITS):
                    n, d = c // ND, c % ND
                    act.wait_ge(xT_ps, m * XT_UNITS + c + 1)
                    act.activation(xT_h[:, d, n * HALF:(n + 1) * HALF], ps[:, bank0 + c, :], ACT.Copy).then_inc(xT_hi, 1)

            act.wait_ge(load["w1"], 16)
            act.activation(w1_q[:, :, :], w1_sb[:, :, :], ACT.Square, accum_out=wss[:, 0:1]).then_inc(wss_ready, 1)
            act.wait_ge(load["w2"], 16)
            act.activation(w2_q[:, :, :], w2_sb[:, :, :], ACT.Square, accum_out=wss[:, 1:2]).then_inc(wss_ready, 1)
            for c in range(XT_UNITS):
                n, d = c // ND, c % ND
                act.wait_ge(ctxT_ps, c + 1)
                act.activation(ctxT_h[:, d, n * HALF:(n + 1) * HALF], ps[:, 4 + c, :], ACT.Copy).then_inc(ctxT_hi, 1)
            norm_high(0, 0)
            act.wait_ge(small_ps, 1)
            act.activation(bqT[:, :], ps[:, 1, 0:NH], ACT.Copy).then_inc(small_ready, 1)

            units = NE0 * ND * NHALF

            def m_high(u):
                act.wait_ge(masked, u + 1)
                if u >= 3:
                    act.wait_ge(down_done, u - 2)
                act.activation(m_h[:, u % 3, :], m_t[:, u % 2, :], ACT.Copy).then_inc(m_hi, 1)

            for u in range(units):
                act.wait_ge(up_done, u + 1)
                if u >= 2:
                    act.wait_ge(gated, u - 1)
                act.activation(m_s[:, u % 2, :], ps[:, u % 4, :], ACT.Silu).then_inc(silu_done, 1)
                if u >= 1:
                    m_high(u - 1)
            m_high(units - 1)

            for c in range(2):
                act.wait_ge(wT_ps, c + 1)
                act.activation(w1T[:, c, :], psb[:, c, :], ACT.Copy).then_inc(wT_ready, 1)
            for c in range(2):
                act.wait_ge(wT_ps, c + 3)
                act.activation(w2T[:, c * NF // 2:(c + 1) * NF // 2, :].rearrange("p a b -> p (a b)"),
                               psb[:, 2 + c, :], ACT.Copy).then_inc(wT_ready, 1)
            act.wait_ge(xqT_ps, 1)
            act.activation(xqT[:, 0, :], psb[:, 4, :], ACT.Copy).then_inc(xqT_ready, 1)

            def hT_copy(t):
                act.wait_ge(hT_ps, t + 1)
                if t >= 2:
                    act.wait_ge(y_ps, t - 1)
                act.activation(hT[:, t % 2, :, :].rearrange("p a b -> p (a b)"), psb[:, 4 + t % 2, :], ACT.Copy).then_inc(hT_ready, 1)

            for t in range(NT):
                act.wait_ge(h_ps, t + 1)
                if t == 0:
                    act.wait_ge(act_scale_ready, 1)
                if t >= 2:
                    act.wait_ge(hq_ready, t - 1)
                act.activation(h_sb[:, t % 2, :], ps[:, 2 * (t % 2):2 * (t % 2) + 2, :].rearrange("p a b -> p (a b)"),
                               ACT.Gelu, scale=adeq[:, t:t + 1]).then_inc(h_ready, 1)
                if t >= 1:
                    hT_copy(t - 1)
            hT_copy(NT - 1)
            norm_high(1, 0)

            def attention(i, k, last_turn):
                g = NSTEP * i

                def live(j):
                    return j >= 0 and not (last_turn and j >= NSTEP)

                j = k - LAG_Q
                if live(j):
                    if j >= 2:
                        wait_alone(act, s_ps, g + j - 1, act_waits)
                    wait_alone(act, q_ps, g + j + 1, act_waits)
                    head = G * i + j % G + G * (j // NSTEP)
                    act.activation(q_h[:, j % 2, :], ps[:, 0, 0:S], ACT.Identity, bias=bqT[:, bass.ds(head, 1)]).then_inc(q_hi, 1)
                    if j >= 1:
                        wait_alone(act, q_ss, g + j, act_waits)
                    act.activation(q_sq[:, :], ps[:, 0, 0:S], ACT.Square, bias=bqT[:, bass.ds(head, 1)]).then_inc(q_squared, 1)
                j = k - LAG_EXP
                if live(j):
                    act.wait_ge(s_max, g + j + 1)
                    for t in range(2):
                        last = act.activation(sc[:, j % 4, t, :], sc[:, j % 4, t, :], ACT.Exp, bias=nmax[:, j % 2, t:t + 1],
                                              accum_out=esum[:, j % 2, t:t + 1])
                    last.then_inc(s_exp, 1)
                j = k - LAG_T
                if live(j):
                    act.wait_ge(pT_ps, g + j + 1)
                    if j >= 2:
                        act.wait_ge(o_ps, g + j - 1)
                    act.activation(pT_h[:, j % 2, :, :].rearrange("p a b -> p (a b)"), ps[:, 4 + j % 2, :], ACT.Copy).then_inc(pT_hi, 1)
                j = k - LAG_PV
                if live(j):
                    act.wait_ge(o_ps, g + j + 1)
                    act.activation(oT_h[:, j % 2, :], ps[:, 6, 0:S], ACT.Copy).then_inc(o_hi, 1)
                b = kv_batch(k - 1)
                if b is not None and not (last_turn and b >= B):
                    act.wait_ge(kv_biased, B * i + b + 1)
                    for t in range(2):
                        last = act.activation(k_sq[:, t, :], kv_sb[:, t, 0:HD], ACT.Square, accum_out=k_ss[:, t:t + 1])
                    last.then_inc(k_squared, 1)
                b = kv_batch(k - 3)
                if b is not None and not (last_turn and b >= B):
                    act.wait_ge(kT_ps, B * i + b + 1)
                    act.activation(kT_h[:, b % B, :], ps[:, 1, 0:S], ACT.Copy).then_inc(kT_hi, 1)

            run_attention(act, attention)
            norm_high(2, 0)

            act.wait_ge(gate_ps, 1)
            act.activation(gs[:, :, 0:NE], ps[:, 0, 0:NT * NE].rearrange("p (t e) -> p t e", e=NE), ACT.Sigmoid).then_inc(gate_sig, 1)

            SU = NS * NHALF
            for u in range(SU + 1):
                if u < SU:
                    act.wait_ge(eg_ps, u + 1)
                    if u >= 2:
                        act.wait_ge(e_lo, u - 1)
                    act.activation(e_s[0:FSH, u % 2, :], ps[0:FSH, 2 * (u % 2), :], ACT.Silu).then_inc(e_silu, 1)
                if u >= 1:
                    j = u - 1
                    act.wait_ge(e_comb, j + 1)
                    if j >= 3:
                        act.wait_ge(e_down, j - 2)
                    act.activation(e_h[0:FSH, j % 3, :], e_s[0:FSH, j % 2, :], ACT.Copy).then_inc(e_hi, 1)
            act.wait_ge(cT_ps, 1)
            act.activation(cT[:, :], psb[0:3 * NE, 0, :], ACT.Copy).then_inc(cT_ready, 1)

            def experts(i, k, last_turn):
                u0 = UNITS * i + SU
                j = k - 1
                if j >= 0 and not (last_turn and j >= UNITS):
                    act.wait_ge(e_comb, u0 + j + 1)
                    act.wait_ge(e_down, u0 + j - 2)
                    act.activation(e_h[:, j % 3, :], e_s[:, j % 2, :], ACT.Copy).then_inc(e_hi, 1)
                if not (last_turn and k >= UNITS):
                    act.wait_ge(eg_ps, u0 + k + 1)
                    act.wait_ge(e_lo, u0 + k - 1)
                    act.activation(e_s[:, k % 2, :], ps[:, 2 * (k % 2), :], ACT.Silu).then_inc(e_silu, 1)

            run_experts(act, experts)
            for n in range(NHALF):
                act.wait_ge(e_down, NG * UPG + SU - 1 + n)
                for d in range(ND):
                    act.activation(yT[:, d, n * HALF:(n + 1) * HALF], ps[:, 4 + ND * n + d, :], ACT.Copy).then_inc(yT_ready, 1)


        @block.vector
        def _(dve):
            step = [0]

            def link(ins):
                step[0] += 1
                ins.then_inc(dve_step, 1)
                dve.wait_ge(dve_step, step[0])

            def stats(t):
                return dve.bn_stats(stat6[:, t, :], x_sb[:, t, :])

            def norm_stats():
                for t in range(NT):
                    last = dve.bn_aggr(mv[:, t, :], stat6[:, t, :])
                link(last)
                dve.tensor_scalar(veps[:, :], mv[:, :, 1], LN_EPS, None, ALU.add).then_inc(stat_ready, 1)

            def norm(n, signal):
                dve.wait_ge(rstd_ready, n + 1)
                for t in range(NT):
                    last = dve.tensor_scalar(xn[:, t, :], x_sb[:, t, :], mv[:, t, 0:1], rstd[:, t:t + 1],
                                             ALU.subtract, ALU.mult)
                    if signal and t % (NT // 2) == NT // 2 - 1:
                        last.then_inc(xn_ready, 1)
                return last

            def norm_low(m, bank0):
                for c in range(XT_UNITS):
                    n, d = c // ND, c % ND
                    tok = slice(n * HALF, (n + 1) * HALF)
                    dve.wait_ge(xT_hi, m * XT_UNITS + c + 1)
                    dve.tensor_tensor(xT_l[:, d, tok], ps[:, bank0 + c, :], xT_h[:, d, tok].bitcast(F32),
                                      ALU.subtract).then_inc(xT_lo, 1)

            for n in range(NHALF):
                dve.wait_ge(load[f"x{n}"], 16)
                for t in range(n * NT // 2, (n + 1) * NT // 2):
                    last = stats(t)
            link(last)
            norm_stats()
            dve.wait_ge(load["itok"], 16)
            above = m_s[:, :, :].rearrange("p a b -> p (a b)")
            dve.tensor_scalar(emask[:, 0, :], itok_sb[:, :], float(SPAN), None, ALU.is_lt)
            for e in range(1, NE0 - 1):
                link(dve.tensor_scalar(above, itok_sb[:, :], float(SPAN * (e + 1)), None, ALU.is_ge))
                link(dve.scalar_tensor_tensor(out=emask[:, e, :], in0=itok_sb[:, :], scalar=float(SPAN * e),
                                              in1=above, op0=ALU.is_ge, op1=ALU.subtract))
            dve.tensor_scalar(emask[:, NE0 - 1, :], itok_sb[:, :], float(SPAN * (NE0 - 1)), None,
                              ALU.is_ge).then_inc(emask_made, 1)
            for c in range(XT_UNITS):
                n, d = c // ND, c % ND
                tok = slice(n * HALF, (n + 1) * HALF)
                dve.wait_ge(ctxT_hi, c + 1)
                dve.tensor_tensor(ctxT_l[:, d, tok], ps[:, 4 + c, :], ctxT_h[:, d, tok].bitcast(F32),
                                  ALU.subtract).then_inc(ctxT_lo, 1)
            norm(0, True)
            norm_low(0, 0)
            dve.wait_ge(wss_ps, 1)
            dve.tensor_scalar(wme[:, :], ps[:, 0, 0:2], 1.0 / (FF * D), Q_EPS, ALU.mult, ALU.max).then_inc(wme_ready, 1)

            w1f = w1_sb[:, :, :].rearrange("p a b -> p (a b)")
            w2f = w2_sb[:, :, :].rearrange("p a b -> p (a b)")
            w1qf = w1_q[:, :, :].rearrange("p a b -> p (a b)")
            w2qf = w2_q[:, :, :].rearrange("p a b -> p (a b)")

            def quantise_weights(n):
                m, op, h = n // 6, n // 2 % 3, n % 2
                w, q = ((w1f, w1qf), (w2f, w2qf))[m]
                c = slice(h * FF, (h + 1) * FF)
                if n == 0:
                    dve.wait_ge(wrms_ready, 1)
                if n >= 2:
                    dve.wait_ge(w_round, n - 1)
                if op == 0:
                    last = dve.tensor_scalar(w[:, c], w[:, c], wrms[:, m:m + 1], 1.0, ALU.mult, ALU.min)
                elif op == 1:
                    last = dve.tensor_scalar(w[:, c], w[:, c], -1.0, MAGIC, ALU.max, ALU.add)
                else:
                    last = dve.tensor_scalar(q[:, c], w[:, c], -MAGIC, None, ALU.add)
                last.then_inc(w_round, 1)

            units = NE0 * ND * NHALF

            def gate_unit(u):
                dve.wait_ge(silu_done, u + 1)
                if u >= 2:
                    dve.wait_ge(m_lo, u - 1)
                dve.tensor_tensor(m_t[:, u % 2, :], m_s[:, u % 2, :], ps[:, u % 4, :], ALU.mult).then_inc(gated, 1)

            def low_unit(u):
                dve.wait_ge(m_hi, u + 1)
                dve.tensor_tensor(m_l[:, u % 3, :], m_t[:, u % 2, :], m_h[:, u % 3, :].bitcast(F32),
                                  ALU.subtract).then_inc(m_lo, 1)

            for u in range(units):
                gate_unit(u)
                if 2 <= u < 14:
                    quantise_weights(u - 2)
                if u >= 1:
                    low_unit(u - 1)
            low_unit(units - 1)
            for c in range(NT // 2):
                dve.wait_ge(down_done, units - 1 + c // 2)
                link(dve.tensor_tensor(x_sb[:, 2 * c:2 * c + 2, :].rearrange("p a b -> p (a b)"),
                                       x_sb[:, 2 * c:2 * c + 2, :].rearrange("p a b -> p (a b)"), ps[:, 4 + c, :], ALU.add))
                stats(2 * c)
                last = stats(2 * c + 1)
            link(last)
            norm_stats()
            link(norm(1, False))
            link(dve.tensor_reduce(amax[:, :], xn[:, :, :], AX.X, ALU.max, apply_absolute_value=True))
            link(dve.tensor_scalar(amax[:, :], amax[:, :], Q_EPS, None, ALU.max))
            link(dve.reciprocal(arec[:, :], amax[:, :]))
            link(dve.tensor_scalar(ascl[:, :], arec[:, :], 127.0, None, ALU.mult))
            dve.tensor_scalar(adeq[:, :], amax[:, :], 1.0 / 127.0, wirms[:, 0:1], ALU.mult, ALU.mult).then_inc(act_scale_ready, 1)
            for t in range(NT):
                last = dve.tensor_scalar(xn[:, t, :], xn[:, t, :], ascl[:, t:t + 1], 127.0, ALU.mult, ALU.min)
            link(last)
            link(dve.tensor_scalar(xn[:, :, :], xn[:, :, :], -128.0, MAGIC, ALU.max, ALU.add))
            dve.wait_ge(wT_ps, 2)
            dve.tensor_scalar(xq[:, :, :], xn[:, :, :], -MAGIC, None, ALU.add).then_inc(xq_ready, 1)
            dve.wait_ge(xqT_ps, 2)
            dve.tensor_copy(xqT[:, 1, :], psb[:, 5, :]).then_inc(xqT_ready, 1)

            def ffn_out(t):
                dve.wait_ge(y_ps, t + 1)
                dve.scalar_tensor_tensor(out=x_sb[:, t, :], in0=ps[:, 6 + t % 2, 0:D], scalar=hdeq[:, t:t + 1],
                                         in1=x_sb[:, t, :], op0=ALU.mult, op1=ALU.add).then_inc(x2_ready, 1)

            for t in range(NT):
                one = slice(t, t + 1)
                dve.wait_ge(h_ready, t + 1)
                link(dve.tensor_reduce(hmax[:, one], h_sb[:, t % 2, :], AX.X, ALU.max, apply_absolute_value=True))
                link(dve.tensor_scalar(hmax[:, one], hmax[:, one], Q_EPS, None, ALU.max))
                link(dve.reciprocal(hrec[:, one], hmax[:, one]))
                link(dve.tensor_scalar(hscl[:, one], hrec[:, one], 127.0, None, ALU.mult))
                dve.tensor_scalar(hdeq[:, one], hmax[:, one], 1.0 / 127.0, wirms[:, 1:2], ALU.mult, ALU.mult)
                link(dve.tensor_scalar(h_sb[:, t % 2, :], h_sb[:, t % 2, :], hscl[:, one], 127.0, ALU.mult, ALU.min))
                dve.tensor_scalar(h_sb[:, t % 2, :], h_sb[:, t % 2, :], -128.0, MAGIC, ALU.max, ALU.add).then_inc(h_round, 1)
                if t >= 2:
                    ffn_out(t - 2)
            for t in range(NT - 2, NT):
                ffn_out(t)
            dve.wait_ge(x2_ready, NT)
            for t in range(NT):
                last = stats(t)
            link(last)
            norm_stats()
            norm(2, True)
            norm_low(1, 0)

            dve.wait_ge(load["mask"], 16)
            dve.wait_ge(load["bkv"], 32)
            dve.wait_ge(knq_made, 1)
            dve.memset(nmax[:, :, :], 0.0).then_inc(y_added, 1)

            def attention(i, k, last_turn):
                g = NSTEP * i

                def live(j):
                    return j >= 0 and not (last_turn and j >= NSTEP)

                j = k - LAG_MAX
                if live(j):
                    dve.wait_ge(s_ps, g + j + 1)
                    dve.wait_ge(q_rs_ready, g + j + 1)
                    if j >= 4:
                        dve.wait_ge(pT_ps, g + j - 3)
                    for t in range(2):
                        last = dve.scalar_tensor_tensor(out=sc[:, j % 4, t, :], in0=ps[:, 2 + j % 2, t * S:(t + 1) * S],
                                                        scalar=q_rs[:, j % 2, t:t + 1], in1=mask_sb[:, t, :],
                                                        op0=ALU.mult, op1=ALU.add)
                    last.then_inc(s_scaled, 1)
                j = k - LAG_Q
                if live(j):
                    head = G * i + j % G + G * (j // NSTEP)
                    dve.wait_ge(q_squared, g + j + 1)
                    dve.scalar_tensor_tensor(out=q_l[:, j % 2, :], in0=ps[:, 0, 0:S], scalar=bqT[:, bass.ds(head, 1)],
                                             in1=q_h[:, j % 2, :].bitcast(F32), op0=ALU.add, op1=ALU.subtract).then_inc(q_lo, 1)
                j = k - LAG_MAX
                if live(j):
                    dve.wait_ge(s_scaled, g + j + 1)
                    dve.tensor_reduce(nmax[:, j % 2, :], sc[:, j % 4, :, :], AX.X, ALU.max, negate=True).then_inc(s_max, 1)
                j = k - LAG_EXP
                if live(j):
                    dve.wait_ge(s_exp, g + j + 1)
                    dve.reciprocal(einv[:, j % 2, :], esum[:, j % 2, :]).then_inc(s_inv, 1)
                j = k - LAG_Q
                if live(j):
                    dve.wait_ge(q_ss, g + j + 1)
                    dve.tensor_scalar(q_ve[:, j % 2, :], ps[:, 0, S:S + 2], HD * RMS_EPS, None, ALU.add).then_inc(q_ve_ready, 1)
                b = kv_batch(k - 1)
                if b is not None and not (last_turn and b >= B):
                    c = B * i + b
                    dve.wait_ge(kv_ps, c + 1)
                    if k > 0:
                        dve.wait_ge(v_split, 2 * c)
                    for t in range(2):
                        last = dve.tensor_tensor(kv_sb[:, t, :].rearrange("p (a h) -> p a h", a=2),
                                                 ps[:, 1, t * 2 * HD:(t + 1) * 2 * HD].rearrange("p (a h) -> p a h", a=2),
                                                 bkv[:, :, bass.ds((i + b // B) * HD, HD)], ALU.add)
                    last.then_inc(kv_biased, 1)
                j = k - LAG_T
                if live(j):
                    dve.wait_ge(pT_hi, g + j + 1)
                    dve.tensor_tensor(pT_l[:, j % 2, :, :].rearrange("p a b -> p (a b)"), ps[:, 4 + j % 2, :],
                                      pT_h[:, j % 2, :, :].rearrange("p a b -> p (a b)").bitcast(F32), ALU.subtract).then_inc(pT_lo, 1)
                j = k - LAG_PV
                if live(j):
                    dve.wait_ge(o_hi, g + j + 1)
                    dve.tensor_tensor(oT_l[:, j % 2, :], ps[:, 6, 0:S], oT_h[:, j % 2, :].bitcast(F32), ALU.subtract).then_inc(o_lo, 1)
                if b is not None and not (last_turn and b >= B):
                    dve.wait_ge(k_squared, c + 1)
                    dve.tensor_scalar(k_ve[:, :], k_ss[:, :], 1.0 / HD, RMS_EPS, ALU.mult, ALU.add).then_inc(k_ve_ready, 1)
                j = k - LAG_WO
                if live(j) and j % G == G - 1:
                    b = j // G
                    dve.wait_ge(wo_used, g + j + 1)
                    xb = x_sb[:, 2 * b:2 * b + 2, :].rearrange("p a b -> p (a b)")
                    dve.tensor_tensor(xb, xb, ps[:, 7, :], ALU.add).then_inc(y_added, 1)
                b = kv_batch(k - 2)
                if b is not None and not (last_turn and b >= B):
                    c = B * i + b
                    dve.wait_ge(k_rs_ready, c + 1)
                    if k > 0:
                        dve.wait_ge(kT_ps, c)
                    for t in range(2):
                        last = dve.scalar_tensor_tensor(out=k_n[:, t, :], in0=kv_sb[:, t, 0:HD], scalar=k_rs[:, t:t + 1],
                                                        in1=knq[:, :], op0=ALU.mult, op1=ALU.mult)
                    last.then_inc(k_normed, 1)
                b = kv_batch(k - 3)
                if b is not None and not (last_turn and b >= B):
                    c = B * i + b
                    dve.wait_ge(kT_hi, c + 1)
                    dve.tensor_tensor(kT_l[:, b % B, :], ps[:, 1, 0:S], kT_h[:, b % B, :].bitcast(F32), ALU.subtract).then_inc(kT_lo, 1)

            run_attention(dve, attention)

            dve.wait_ge(y_added, B * NKV + 1)
            for t in range(NT):
                last = stats(t)
            link(last)
            norm_stats()
            norm(3, True)
            norm_low(2, 0)
            dve.memset(gs[:, :, NE:NE + 2], -1.0)
            dve.wait_ge(gate_sig, 1)
            for t in range(NT):
                last = dve.max(gtop[:, t, :], gs[:, t, 0:NE])
            link(last)
            link(dve.tensor_reduce(gsum[:, :], gtop[:, :, 0:TOPK], AX.X, ALU.add))
            link(dve.memset(gtop[:, :, TOPK:8], -1.0))
            for t in range(NT):
                last = dve.match_replace(out=grep[:, t, :], in_to_replace=gtop[:, t, :], in_values=gs[:, t, :], imm_value=0.0)
            link(dve.tensor_scalar(gsum[:, :], gsum[:, :], 1e-20, None, ALU.add))
            link(dve.reciprocal(grec[:, :], gsum[:, :]))
            link(dve.tensor_tensor(gc[:, :, :], gs[:, :, 0:NE], grep[:, :, 0:NE], ALU.subtract))
            link(dve.tensor_tensor(gc[:, :, :], gc[:, :, :], grec[:, :].unsqueeze(2).broadcast_to([P, NT, NE]), ALU.mult))
            for part in range(3):
                last = dve.tensor_copy(gparts[:, :, part, :], gc[:, :, :])
                if part < 2:
                    link(last)
                    link(dve.tensor_tensor(gc[:, :, :], gc[:, :, :], gparts[:, :, part, :], ALU.subtract))
            last.then_inc(parts_ready, 1)

            SU = NS * NHALF
            for u in range(SU + 1):
                if u >= 1:
                    j = u - 1
                    dve.wait_ge(e_hi, j + 1)
                    dve.tensor_tensor(e_l[0:FSH, j % 3, :], e_s[0:FSH, j % 2, :], e_h[0:FSH, j % 3, :].bitcast(F32),
                                      ALU.subtract).then_inc(e_lo, 1)
                if u < SU:
                    dve.wait_ge(e_silu, u + 1)
                    dve.wait_ge(eu_ps, u + 1)
                    dve.tensor_tensor(e_s[0:FSH, u % 2, :], e_s[0:FSH, u % 2, :], ps[0:FSH, 2 * (u % 2) + 1, :],
                                      ALU.mult).then_inc(e_comb, 1)

            def experts(i, k, last_turn):
                u0 = UNITS * i + SU
                j = k - 1
                if j >= 0 and not (last_turn and j >= UNITS):
                    dve.wait_ge(e_hi, u0 + j + 1)
                    dve.tensor_tensor(e_l[:, j % 3, :], e_s[:, j % 2, :], e_h[:, j % 3, :].bitcast(F32), ALU.subtract).then_inc(e_lo, 1)
                if not (last_turn and k >= UNITS):
                    dve.wait_ge(e_silu, u0 + k + 1)
                    dve.wait_ge(eu_ps, u0 + k + 1)
                    dve.tensor_tensor(e_s[:, k % 2, :], e_s[:, k % 2, :], ps[:, 2 * (k % 2) + 1, :], ALU.mult).then_inc(e_mult, 1)
                    dve.wait_ge(e_mult, UNITS * i + k + 1)
                    dve.wait_ge(ec_ps, UNITS * i + k + 1)
                    dve.tensor_tensor(e_s[:, k % 2, :], e_s[:, k % 2, :], ps[:, 2 * (k % 2), :], ALU.mult).then_inc(e_comb, 1)

            run_experts(dve, experts)
            for n in range(NT // 2):
                dve.wait_ge(yb_ps, n + 1)
                xb = x_sb[:, 2 * n:2 * n + 2, :].rearrange("p a b -> p (a b)")
                dve.tensor_tensor(xb, xb, ps[:, n, :], ALU.add).then_inc(out_ready, 1)


_INS = ['x', 'itok_BxS_13_99985', 'ctx_2048', 'mask_1xSxS2_ff0', 'L0_ffn_w1', 'L0_ffn_w2', 'L1_xattn_Wq', 'L1_xattn_bq',
        'L1_xattn_Wk', 'L1_xattn_bk', 'L1_xattn_Wv', 'L1_xattn_bv', 'L1_xattn_Wo', 'L1_xattn_qn_w', 'L1_xattn_kn_w',
        'L1_ffn_gate_w', 'L1_ffn_wg', 'L1_ffn_wu', 'L1_ffn_wd', 'L1_ffn_sg', 'L1_ffn_su', 'L1_ffn_sd']
_OUTS = [((4, 256, 256), 'float32')]


def kernel(**inputs):
    import numpy as _np
    import concourse.bacc as _bacc
    from concourse import mybir as _mybir
    from concourse.bass_utils import run_bass_kernel_spmd as _run

    nc = _bacc.Bacc("TRN2", target_bir_lowering=False, num_devices=1)
    arrays, args = {}, []
    for name in _INS:
        a = _np.ascontiguousarray(inputs[name])
        arrays[f"in_{name}_dram"] = a
        args.append(nc.dram_tensor(f"in_{name}_dram", a.shape, _mybir.dt.from_np(a.dtype), kind="ExternalInput").ap())
    for i, (shape, dtype) in enumerate(_OUTS):
        dt = _mybir.dt.from_np(_np.dtype(dtype))
        args.append(nc.dram_tensor(f"out_{i}_dram", shape, dt, kind="ExternalOutput").ap())
    build_program(nc, *args)
    r = _run(nc, [arrays], core_ids=[0])
    return r.results[0]["out_0_dram"]
```

```python
from contextlib import ExitStack

import concourse.bass as bass
from concourse import mybir

F32 = mybir.dt.float32
F32R = mybir.dt.float32r
BF16 = mybir.dt.bfloat16
I32 = mybir.dt.int32
ALU = mybir.AluOpType
ACT = mybir.ActivationFunctionType
AX = mybir.AxisListType

P = 128
MAGIC = 12582912.0


def build_program(nc, x, itok, ctx_in, mask_in, w1, w2, Wq, bq, Wk, bk, Wv, bv, Wo, qn_w, kn_w,
                  gate_w, wg, wu, wd, sg, su, sd, out):
    B, S, D = x.shape
    T = B * S
    NT = T // P
    ND = D // P
    NE0 = ctx_in.shape[0]
    SPAN = 12500 // NE0
    FF = w1.shape[0]
    NF = FF // P
    HD = qn_w.shape[0]
    NKV = Wk.shape[1] // HD
    NH = Wq.shape[1] // HD
    G = NH // NKV
    NE, _, FE = wg.shape
    FS = sg.shape[1]
    TOPK = 6
    HALF = T // 2
    NHALF = 2
    LN_EPS, Q_EPS, RMS_EPS = 1e-5, 1e-5, 1e-6

    with ExitStack() as ctx:
        stacks = [ctx]

        def sb(name, shape, dt=F32):
            return stacks[-1].enter_context(nc.sbuf_tensor(name, shape, dt))

        def sem(name):
            return ctx.enter_context(nc.semaphore(name))

        x_sb = sb("x_sb", [P, NT, D])
        xn = sb("xn", [P, NT, D])
        xT_h = sb("xT_h", [P, ND, T], F32R)
        xT_l = sb("xT_l", [P, ND, T], F32R)
        ctxT_h = sb("ctxT_h", [P, ND, T], F32R)
        ctxT_l = sb("ctxT_l", [P, ND, T], F32R)
        ident = sb("ident", [P, P])
        identb = sb("identb", [P, P], BF16)
        ones = sb("ones", [P, P])
        neg_half = sb("neg_half", [P, 2])
        neg_magic = sb("neg_magic", [P, 1])
        pos_half = sb("pos_half", [P, 2])
        stat6 = sb("stat6", [P, NT, 6])
        mv = sb("mv", [P, NT, 2])
        veps = sb("veps", [P, NT])
        rstd = sb("rstd", [P, NT])
        mask_sb = sb("mask_sb", [P, S // P, S])
        smalls = sb("smalls", [NH + 2, HD])
        bqT = sb("bqT", [P, NH])
        bkv = sb("bkv", [P, 2, NKV * HD])
        knq = sb("knq", [P, HD])
        gw_r = sb("gw_r", [P, ND, NE])
        gw_h = sb("gw_h", [P, ND, NE], F32R)
        gw_l = sb("gw_l", [P, ND, NE], F32R)

        ps = ctx.enter_context(nc.psum_tensor("ps", [P, 8, 512], F32))
        psb = ps[:, :, :].rearrange("p a b -> p (a b)").bitcast(BF16).rearrange("p (a b) -> p a b", a=8)

        wq_r = sb("wq_r", [P, ND, G * HD])
        wkv_r = sb("wkv_r", [P, ND, 2 * HD])
        wo_r = sb("wo_r", [P, G, D])
        wq_h = sb("wq_h", [P, ND, G * HD], F32R)
        wq_l = sb("wq_l", [P, ND, G * HD], F32R)
        wkv_h = sb("wkv_h", [P, ND, 2 * HD], F32R)
        wkv_l = sb("wkv_l", [P, ND, 2 * HD], F32R)
        wo_h = sb("wo_h", [P, G, D], F32R)
        wo_l = sb("wo_l", [P, G, D], F32R)
        kv_sb = sb("kv_sb", [P, 2, 2 * HD])
        k_sq = sb("k_sq", [P, 2, HD])
        k_ss = sb("k_ss", [P, 2])
        k_ve = sb("k_ve", [P, 2])
        k_rs = sb("k_rs", [P, 2])
        k_n = sb("k_n", [P, 2, HD])
        qnb = k_n[:, 0, :]
        kT_h = sb("kT_h", [P, B, S], F32R)
        kT_l = sb("kT_l", [P, B, S], F32R)
        v_h = sb("v_h", [P, B, 2, HD], F32R)
        v_l = sb("v_l", [P, B, 2, HD], F32R)
        q_h = sb("q_h", [P, 2, S], F32R)
        q_l = sb("q_l", [P, 2, S], F32R)
        q_sq = sb("q_sq", [P, S])
        q_ve = sb("q_ve", [P, 2, 2])
        q_rs = sb("q_rs", [P, 2, 2])
        sc = sb("sc", [P, 4, 2, S])
        nmax = sb("nmax", [P, 2, 2])
        esum = sb("esum", [P, 2, 2])
        einv = sb("einv", [P, 2, 2])
        pT_h = sb("pT_h", [P, 2, 2, S], F32R)
        pT_l = sb("pT_l", [P, 2, 2, S], F32R)
        oT_h = sb("oT_h", [P, 2, S], F32R)
        oT_l = sb("oT_l", [P, 2, S], F32R)

        layer0 = ExitStack()
        stacks.append(layer0)
        ctx_sb = sb("ctx_sb", [P, NT, D])
        itok_sb = sb("itok_sb", [P, T], I32)
        emask = sb("emask", [P, NE0, T], BF16)
        m_s = sb("m_s", [P, 2, HALF])
        m_t = sb("m_t", [P, 2, HALF])
        m_h = sb("m_h", [P, 3, HALF], F32R)
        m_l = sb("m_l", [P, 3, HALF], F32R)
        w1_sb = sb("w1_sb", [P, NF, D])
        w2_sb = sb("w2_sb", [P, ND, FF])
        wss = sb("wss", [P, 2])
        wme = sb("wme", [P, 2])
        wrms = sb("wrms", [P, 2])
        wirms = sb("wirms", [P, 2])
        w1_q = sb("w1_q", [P, NF, D], BF16)
        w2_q = sb("w2_q", [P, ND, FF], BF16)
        w1T = sb("w1T", [P, ND, FF], BF16)
        w2T = sb("w2T", [P, NF, D], BF16)
        amax = sb("amax", [P, NT])
        arec = sb("arec", [P, NT])
        ascl = sb("ascl", [P, NT])
        adeq = sb("adeq", [P, NT])
        xq = w1_q
        xqT = sc[:, 0:2, :, :].rearrange("p a b c -> p (a b c)").bitcast(BF16).rearrange("p (d t) -> p d t", d=ND)
        h_slots = [m[:, :, :].rearrange("p a b -> p (a b)").rearrange("p (a b) -> p a b", a=2)[:, half, :]
                   for m in (ctx_sb, w1_sb, w2_sb) for half in range(2)]
        HS = len(h_slots)
        H_LAG = 2
        H_LEAD = 4
        h_q = m_s[:, :, :].rearrange("p a b -> p (a b)").bitcast(BF16).rearrange("p (a b) -> p a b", a=2)
        hT = m_t[:, :, :].rearrange("p a b -> p (a b)").bitcast(BF16).rearrange("p (a f t) -> p a f t", a=2, f=NF)
        hmax = sb("hmax", [P, NT])
        hrec = sb("hrec", [P, NT])
        hscl = sb("hscl", [P, NT])
        hdeq = sb("hdeq", [P, NT])
        stacks.pop()
        layer0.close()

        EG = 4
        GF = EG * FE
        JT = GF // P
        NG = NE // EG
        M_LAG = 3
        WSS_BANK = 2
        WEIGHT_UNITS = (4, 6, 7, 9, 11, 12, 14)
        WSS_UNIT = 5
        cT = sb("cT", [NE, T])
        c_dram = nc.dram_tensor("combine_weights", [NE, T], F32, kind="Internal").ap()
        comb = [[w[:, :, :].bitcast(F32).rearrange("p a b -> p (a b)") for w in ws]
                for ws in ((wq_h, wq_l, wo_h), (wo_l, wq_r, wo_r))]
        wg_r = sb("wg_r", [P, ND, GF])
        wu_r = sb("wu_r", [P, ND, GF])
        wd_r = sb("wd_r", [P, JT, D])
        wg_h = sb("wg_h", [P, 2, ND, GF], F32R)
        wg_l = sb("wg_l", [P, 2, ND, GF], F32R)
        wu_h = sb("wu_h", [P, 2, ND, GF], F32R)
        wu_l = sb("wu_l", [P, 2, ND, GF], F32R)
        wd_h = sb("wd_h", [P, 2, JT, D], F32R)
        wd_l = sb("wd_l", [P, 2, JT, D], F32R)
        e_s = sb("e_s", [P, 2, HALF])
        e_h, e_l = (c[:, :, :].rearrange("p a b -> p (a b)")[:, 0:3 * HALF].rearrange("p (a b) -> p a b", a=3)
                    for c in (ctxT_h, ctxT_l))
        NS = 2
        FSH = FS // NS
        sgu_r = sb("sgu_r", [P, 2, ND, FS])
        sd_r = sb("sd_r", [FSH, NS, D])
        sgu_h, sgu_l = (w[:, 1, :, :].rearrange("p a b -> p (a b)").rearrange("p (m d f) -> p m d f", m=2, d=ND)
                        for w in (wg_h, wg_l))
        sd_h, sd_l = (w[0:FSH, 1, 0:NS, :] for w in (wd_h, wd_l))
        gs = sb("gs", [P, NT, NE + 2])
        grep = sb("grep", [P, NT, NE + 2])
        gtop = sb("gtop", [P, NT, 8])
        gsum = sb("gsum", [P, NT])
        grec = sb("grec", [P, NT])
        gc = sb("gc", [P, NT, NE])
        yT = xn[:, :, :].rearrange("p a b -> p (a b)").rearrange("p (d t) -> p d t", d=ND)

        load = {n: sem("ld_" + n) for n in ("x0", "x1", "ctx0", "ctx1", "itok", "w1", "w2", "small", "bkv", "knq", "mask", "gate",
                                            "wq", "wkv", "wo", "moe", "shared", "comb0", "comb1")}
        consts_made = sem("consts_made")
        pool_step = sem("pool_step")
        dve_step = sem("dve_step")
        act_step = sem("act_step")
        stat_ready = sem("stat_ready")
        rstd_ready = sem("rstd_ready")
        xn_ready = sem("xn_ready")
        xT_ps = sem("xT_ps")
        xT_hi = sem("xT_hi")
        xT_lo = sem("xT_lo")
        ctxT_ps = sem("ctxT_ps")
        ctxT_hi = sem("ctxT_hi")
        ctxT_lo = sem("ctxT_lo")
        emask_made = sem("emask_made")
        up_done = sem("up_done")
        silu_done = sem("silu_done")
        gated = sem("gated")
        masked = sem("masked")
        m_hi = sem("m_hi")
        m_lo = sem("m_lo")
        down_done = sem("down_done")
        x1_ready = sem("x1_ready")
        wss_ready = sem("wss_ready")
        wss_ps = sem("wss_ps")
        wme_ready = sem("wme_ready")
        wrms_ready = sem("wrms_ready")
        wT_ps = sem("wT_ps")
        wT_ready = sem("wT_ready")
        xq_ready = sem("xq_ready")
        xqT_ps = sem("xqT_ps")
        xqT_ready = sem("xqT_ready")
        h_ps = sem("h_ps")
        h_ready = sem("h_ready")
        h_integers = sem("h_integers")
        hq_ready = sem("hq_ready")
        hT_ps = sem("hT_ps")
        hT_ready = sem("hT_ready")
        y_ps = sem("y_ps")
        x2_ready = sem("x2_ready")
        small_ready = sem("small_ready")
        knq_made = sem("knq_made")

        kv_split = sem("kv_split")
        wq_split = sem("wq_split")
        wo_split = sem("wo_split")
        kv_ps = sem("kv_ps")
        kv_biased = sem("kv_biased")
        k_squared = sem("k_squared")
        k_ve_ready = sem("k_ve_ready")
        k_rs_ready = sem("k_rs_ready")
        k_normed = sem("k_normed")
        v_hi = sem("v_hi")
        v_lo = sem("v_lo")
        kv_hi = sem("kv_weights_hi")
        kT_ps = sem("kT_ps")
        kT_hi = sem("kT_hi")
        kT_lo = sem("kT_lo")
        q_ps = sem("q_ps")
        q_hi = sem("q_hi")
        q_squared = sem("q_squared")
        q_lo = sem("q_lo")
        q_ss = sem("q_ss")
        q_ve_ready = sem("q_ve_ready")
        q_rs_ready = sem("q_rs_ready")
        s_ps = sem("s_ps")
        s_scaled = sem("s_scaled")
        s_max = sem("s_max")
        s_exp = sem("s_exp")
        s_inv = sem("s_inv")
        s_normed = sem("s_normed")
        pT_ps = sem("pT_ps")
        pT_hi = sem("pT_hi")
        pT_lo = sem("pT_lo")
        o_ps = sem("o_ps")
        o_hi = sem("o_hi")
        o_lo = sem("o_lo")
        y_done = sem("y_done")
        y_added = sem("y_added")
        wo_used = sem("wo_used")

        gw_split = sem("gw_split")
        shared_split = sem("shared_split")
        moe_split = sem("moe_split")
        c_stored = sem("combine_weights_stored")
        gate_ps = sem("gate_ps")
        gate_sig = sem("gate_sig")
        c_ready = sem("combine_weights_ready")
        cT_ps = sem("cT_ps")
        cT_ready = sem("cT_ready")
        eg_ps = sem("eg_ps")
        eu_ps = sem("eu_ps")
        e_silu = sem("e_silu")
        e_mult = sem("e_mult")
        e_comb = sem("e_comb")
        e_hi = sem("e_hi")
        e_lo = sem("e_lo")
        e_down = sem("e_down")
        yT_ready = sem("yT_ready")
        yb_ps = sem("yb_ps")
        out_ready = sem("out_ready")
        stored = sem("stored")

        chain = sem("pool_attention_step")
        moe_chain = sem("pool_expert_step")
        act_scale_ready = sem("act_scale_ready")
        x_scale_ready = sem("x_scale_ready")
        x_rounded = sem("x_rounded")
        x_integers = sem("x_integers")
        h_scale_ready = sem("h_scale_ready")
        h_rounded = sem("h_rounded")
        w_round = sem("w_round")
        pool_waits = sem("pool_waits")
        act_waits = sem("act_waits")

        NPAIR = NT // 2
        XT_BANKS = ((0, 1, 2, 3), (0, 2, 3, 4), (1, 1, 1, 3))
        CTX_UNITS = NHALF * ND

        def three(pe, dst, wh, wl, vh, vl, start, stop, **kw):
            pe.matmul(dst, wh, vh, start=start, stop=False, **kw)
            pe.matmul(dst, wh, vl, start=False, stop=False, **kw)
            return pe.matmul(dst, wl, vh, start=False, stop=stop, **kw)

        block = ctx.enter_context(nc.Block())

        LAG_Q, LAG_S, LAG_MAX, LAG_EXP, LAG_T, LAG_PV, LAG_WO = 1, 2, 3, 4, 5, 6, 7
        NSTEP = B * G
        FIRST = LAG_WO
        UPG = JT * NHALF
        UNITS = 2 * UPG
        LAG_DOWN = 2
        COMB_DMAS = JT + EG - 1

        def added_batch(k):
            j = k - LAG_WO
            return j // G if j >= 0 and j % G == G - 1 else None

        KV_LEAD = 5
        WO_LATE = (7,)
        KV_SPLIT = 10
        PREPARE = (9, 10, 12, 13, 14, 15)
        Q_SPLIT = (14, 15, 17, 18)
        WO_EARLY = (20, 21, 22)
        GATE_STEPS = [LAG_S + NSTEP, LAG_S + NSTEP + 1, LAG_WO + NSTEP - 1]

        def kv_batch(k):
            return (k + KV_LEAD) // G if (k + KV_LEAD) % G == 0 else None

        @block.sync
        def _(sp):
            x_v = x.rearrange("b (t p) d -> p (b t) d", p=P)
            for n in range(NHALF):
                sp.dma_start(x_sb[:, n * NT // 2:(n + 1) * NT // 2, :],
                             x_v[:, n * NT // 2:(n + 1) * NT // 2, :]).then_inc(load[f"x{n}"], 16)
            ctx_v = ctx_in.rearrange("b (t p) d -> p (b t) d", p=P)
            for n in range(NHALF):
                sp.dma_start(ctx_sb[:, n * NT // 2:(n + 1) * NT // 2, :],
                             ctx_v[:, n * NT // 2:(n + 1) * NT // 2, :]).then_inc(load[f"ctx{n}"], 16)
            sp.dma_start(itok_sb[:, :], itok.rearrange("b s -> (b s)").unsqueeze(0).broadcast_to([P, T])).then_inc(load["itok"], 16)
            sp.dma_start(w1_sb[:, :, :], w1.rearrange("(t p) d -> p t d", p=P)).then_inc(load["w1"], 16)
            sp.dma_start(w2_sb[:, :, :], w2.rearrange("(t p) d -> p t d", p=P)).then_inc(load["w2"], 16)
            sp.dma_start(smalls[0:NH, :], bq.rearrange("(h d) -> h d", d=HD)).then_inc(load["small"], 16)
            sp.dma_start(smalls[NH:NH + 1, :], qn_w.unsqueeze(0)).then_inc(load["small"], 16)
            sp.dma_start(smalls[NH + 1:NH + 2, :], kn_w.unsqueeze(0)).then_inc(load["small"], 16)
            sp.dma_start(bkv[:, 0, :], bk.unsqueeze(0).broadcast_to([P, NKV * HD])).then_inc(load["bkv"], 16)
            sp.dma_start(bkv[:, 1, :], bv.unsqueeze(0).broadcast_to([P, NKV * HD])).then_inc(load["bkv"], 16)
            sp.dma_start(qnb, qn_w.unsqueeze(0).broadcast_to([P, HD])).then_inc(load["knq"], 16)
            sp.dma_start(knq[:, :], kn_w.unsqueeze(0).broadcast_to([P, HD])).then_inc(load["knq"], 16)
            sp.dma_start(mask_sb[:, :, :], mask_in[0].rearrange("(t p) k -> p t k", p=P)).then_inc(load["mask"], 16)
            sp.dma_start(gw_r[:, :, :], gate_w.rearrange("(t p) e -> p t e", p=P)).then_inc(load["gate"], 16)

            def load_heads(kv, after):
                if after:
                    sp.wait_ge(kv_split, kv)
                sp.dma_start(wkv_r[:, :, 0:HD], Wk.rearrange("(t p) n -> p t n", p=P)[:, :, bass.ds(kv * HD, HD)]).then_inc(load["wkv"], 16)
                sp.dma_start(wkv_r[:, :, HD:2 * HD], Wv.rearrange("(t p) n -> p t n", p=P)[:, :, bass.ds(kv * HD, HD)]).then_inc(load["wkv"], 16)
                if after:
                    sp.wait_ge(wq_split, kv * G)
                sp.dma_start(wq_r[:, :, :], Wq.rearrange("(t p) n -> p t n", p=P)[:, :, bass.ds(kv * G * HD, G * HD)]).then_inc(load["wq"], 16)
                if after:
                    sp.wait_ge(wo_split, kv * G)
                sp.dma_start(wo_r[:, :, :], Wo.rearrange("(h p) n -> p h n", p=P)[:, bass.ds(kv * G, G), :]).then_inc(load["wo"], 16)

            load_heads(0, False)
            sp.wait_ge(x2_ready, NT)
            for n, w in enumerate((sg, su)):
                sp.dma_start(sgu_r[:, n, :, :], w.rearrange("(t p) f -> p t f", p=P)).then_inc(load["shared"], 16)
            sp.dma_start(sd_r[:, :, :], sd.rearrange("(t p) d -> p t d", p=FSH)).then_inc(load["shared"], 16)

            wd_v = wd.rearrange("e f d -> (e f) d").rearrange("(j p) d -> p j d", p=P)

            def load_experts(g):
                for t in range(ND):
                    sp.dma_start(wg_r[:, t, :].rearrange("p (e f) -> p e f", f=FE),
                                 wg[bass.ds(g * EG, EG), t * P:(t + 1) * P, :].rearrange("e p f -> p e f")).then_inc(load["moe"], 16)
                    sp.dma_start(wu_r[:, t, :].rearrange("p (e f) -> p e f", f=FE),
                                 wu[bass.ds(g * EG, EG), t * P:(t + 1) * P, :].rearrange("e p f -> p e f")).then_inc(load["moe"], 16)
                sp.dma_start(wd_r[:, :, :], wd_v[:, bass.ds(g * JT, JT), :]).then_inc(load["moe"], 16)

            load_experts(0)
            with sp.Fori(1, NKV) as kv:
                load_heads(kv, True)

            def load_combine(g, slot):
                for j in range(JT):
                    for e in range(EG):
                        lo, hi = max(j * P, e * FE), min((j + 1) * P, (e + 1) * FE)
                        if lo < hi:
                            sp.dma_start(comb[slot][j][lo - j * P:hi - j * P, :],
                                         c_dram[bass.ds(g * EG + e, 1), :].broadcast_to([hi - lo, T])).then_inc(load[f"comb{slot}"], 16)

            sp.wait_ge(moe_split, 6)
            load_experts(1)
            sp.wait_ge(cT_ready, 1)
            sp.dma_start(c_dram[:, :], cT[:, :]).then_inc(c_stored, 16)
            sp.wait_ge(c_stored, 16)
            for g in range(2):
                load_combine(g, g)
            with sp.Fori(1, NG // 2) as i:
                for slot in range(2):
                    sp.wait_ge(moe_split, 6 * (2 * i + slot))
                    load_experts(2 * i + slot)
                    sp.wait_ge(e_comb, NS * NHALF + (2 * i + slot - 1) * UPG)
                    load_combine(2 * i + slot, slot)

            out_v = out.rearrange("b (t p) d -> p (b t) d", p=P)
            for n in range(NT // 2):
                sp.wait_ge(out_ready, n + 1)
                sp.dma_start(out_v[:, 2 * n:2 * n + 2, :], x_sb[:, 2 * n:2 * n + 2, :]).then_inc(stored, 16)
            sp.wait_ge(stored, 16 * (NT // 2))

        def wait_alone(eng, semaphore, value, passed):
            eng.wait_ge(semaphore, value)
            if not isinstance(value, int):
                eng.sem_inc(passed, 1)

        def run_attention(eng, body):
            for k in range(FIRST):
                body(0, k, False)
            with eng.Fori(0, NKV - 1) as i:
                for k in range(FIRST, FIRST + NSTEP):
                    body(i, k, False)
            for k in range(FIRST, FIRST + NSTEP):
                body(NKV - 1, k, True)

        def run_experts(eng, body):
            for k in range(LAG_DOWN):
                body(0, k, False)
            with eng.Fori(0, NG // 2 - 1) as i:
                for k in range(LAG_DOWN, LAG_DOWN + UNITS):
                    body(i, k, False)
            for k in range(LAG_DOWN, LAG_DOWN + UNITS):
                body(NG // 2 - 1, k, True)

        @block.gpsimd
        def _(pool):
            step = [0]

            def link(ins):
                step[0] += 1
                ins.then_inc(pool_step, 1)
                pool.wait_ge(pool_step, step[0])

            link(pool.memset(ident[:, :], 0.0))
            link(pool.affine_select(out=ident[:, :], in_=ident[:, :], compare_op=ALU.not_equal, fill=1.0, base=0,
                                    pattern=[[-1, P]], channel_multiplier=1))
            pool.memset(neg_half[:, :], -0.5)
            pool.memset(pos_half[:, :], 0.5)
            pool.memset(ones[:, :], 1.0)
            pool.tensor_copy(identb[:, :], ident[:, :])

            pool.memset(neg_magic[:, :], -MAGIC).then_inc(consts_made, 1)
            pool.wait_ge(consts_made, 1)

            def norm_scale(n, c):
                pool.wait_ge(stat_ready, n * NPAIR + c + 1)
                pool.tensor_tensor(rstd[:, 2 * c:2 * c + 2], veps[:, 2 * c:2 * c + 2], neg_half[:, 0:2],
                                   ALU.pow).then_inc(rstd_ready, 1)

            def split(h, l, r, done):
                step[0] += 1
                pool.tensor_copy(h, r).then_inc(pool_step, 1)
                pool.wait_ge(pool_step, step[0])
                pool.tensor_tensor(l, r, h.bitcast(F32), ALU.subtract).then_inc(done, 1)

            def first_weights(n):
                if n == 0:
                    pool.wait_ge(load["wkv"], 32)
                    split(wkv_h[:, :, :], wkv_l[:, :, :], wkv_r[:, :, :], kv_split)
                elif n == 1:
                    pool.wait_ge(load["gate"], 16)
                    split(gw_h[:, :, :], gw_l[:, :, :], gw_r[:, :, :], gw_split)
                    pool.wait_ge(load["knq"], 32)
                    pool.tensor_tensor(knq[:, :], knq[:, :], qnb, ALU.mult).then_inc(knq_made, 1)
                elif n < 2 + G:
                    h = n - 2
                    if h == 0:
                        pool.wait_ge(load["wq"], 16)
                    split(wq_h[:, :, h * HD:(h + 1) * HD], wq_l[:, :, h * HD:(h + 1) * HD],
                          wq_r[:, :, h * HD:(h + 1) * HD], wq_split)
                elif n < 2 + G + len(WO_EARLY):
                    h = n - 2 - G
                    if h == 0:
                        pool.wait_ge(load["wo"], 16)
                    split(wo_h[:, h, :], wo_l[:, h, :], wo_r[:, h, :], wo_split)

            for c in range(NPAIR):
                norm_scale(0, c)
            for u in range(NE0 * ND * NHALF):
                e, n = u // (ND * NHALF), u % NHALF
                pool.wait_ge(gated, u + 1)
                if u % (ND * NHALF) == 0:
                    pool.wait_ge(emask_made, e + 1)
                pool.tensor_tensor(m_t[:, u % 2, :], m_t[:, u % 2, :], emask[:, e, n * HALF:(n + 1) * HALF],
                                   ALU.mult).then_inc(masked, 1)
                if u == WSS_UNIT:
                    pool.wait_ge(wme_ready, 1)
                    pool.tensor_tensor(wrms[:, :], wme[:, :], neg_half[:, 0:2], ALU.pow)
                    pool.tensor_tensor(wirms[:, :], wme[:, :], pos_half[:, :], ALU.pow).then_inc(wrms_ready, 1)
                if u in WEIGHT_UNITS:
                    first_weights(WEIGHT_UNITS.index(u))

            for c in range(NPAIR + 1):
                if c < NPAIR:
                    norm_scale(1, c)
                if c >= 1:
                    pool.wait_ge(x_scale_ready, c)
                    for t in range(2 * c - 2, 2 * c):
                        last = pool.tensor_scalar(xn[:, t, :], xn[:, t, :], ascl[:, t:t + 1], MAGIC, ALU.mult, ALU.add)
                    last.then_inc(x_rounded, 1)

            for n in range(len(WEIGHT_UNITS), 2 + G + len(WO_EARLY)):
                first_weights(n)
            for t in range(NT):
                pool.wait_ge(h_scale_ready, t + 1)
                pool.tensor_scalar(h_slots[t % HS], h_slots[t % HS], hscl[:, t:t + 1], MAGIC, ALU.mult, ALU.add).then_inc(h_rounded, 1)
                pool.wait_ge(h_rounded, t + 1)
                if t >= 2:
                    pool.wait_ge(hT_ps, t - 1)
                pool.tensor_scalar(h_q[:, t % 2, :], h_slots[t % HS], 1.0, -MAGIC, ALU.mult, ALU.add).then_inc(h_integers, 1)
            norm_scale(2, 0)

            def split_in_loop(h, l, r, done, value):
                pool.tensor_copy(h, r).then_inc(chain, 1)
                pool.wait_ge(chain, value)
                pool.tensor_tensor(l, r, h.bitcast(F32), ALU.subtract).then_inc(done, 1)

            def attention(i, k, last):
                def live(j):
                    return j >= 0 and not (last and j >= NSTEP)

                if last and added_batch(k - 2) is not None:
                    norm_scale(3, added_batch(k - 2))
                j = k - LAG_EXP
                if live(j):
                    wait_alone(pool, s_inv, NSTEP * i + j + 1, pool_waits)
                    for t in range(2):
                        pool.tensor_scalar(sc[:, j % 4, t, :], sc[:, j % 4, t, :], einv[:, j % 2, t:t + 1], 1.0,
                                           ALU.mult, ALU.mult).then_inc(s_normed, 1)
                j = k - LAG_Q
                if live(j):
                    pool.wait_ge(q_ve_ready, NSTEP * i + j + 1)
                    pool.tensor_tensor(q_rs[:, j % 2, :], q_ve[:, j % 2, :], neg_half[:, 0:2], ALU.pow).then_inc(q_rs_ready, 1)
                b = kv_batch(k - 2)
                if b is not None and not (last and b >= B):
                    pool.wait_ge(k_ve_ready, B * i + b + 1)
                    pool.tensor_tensor(k_rs[:, :], k_ve[:, :], neg_half[:, 0:2], ALU.pow).then_inc(k_rs_ready, 1)
                b = kv_batch(k - 3)
                if b is not None and not (last and b >= B):
                    pool.wait_ge(v_hi, B * i + b + 1)
                    pool.tensor_tensor(v_l[:, b % B, :, :], kv_sb[:, :, HD:2 * HD], v_h[:, b % B, :, :].bitcast(F32),
                                       ALU.subtract).then_inc(v_lo, 1)
                if k in WO_LATE:
                    h = len(WO_EARLY) + WO_LATE.index(k)
                    if h == len(WO_EARLY):
                        wait_alone(pool, load["wo"], 16 * i + 16, pool_waits)
                        wait_alone(pool, y_added, B * i + 1, pool_waits)
                    split_in_loop(wo_h[:, h, :], wo_l[:, h, :], wo_r[:, h, :], wo_split, 8 * i + 1 + WO_LATE.index(k))
                if last:
                    if k in PREPARE:
                        expert_preparations(PREPARE.index(k))
                    return
                if k < FIRST:
                    return
                if k == KV_SPLIT:
                    pool.wait_ge(kv_hi, i + 1)
                    pool.tensor_tensor(wkv_l[:, :, :], wkv_r[:, :, :], wkv_h[:, :, :].bitcast(F32), ALU.subtract).then_inc(kv_split, 1)
                if k in Q_SPLIT:
                    h = Q_SPLIT.index(k)
                    if h == 0:
                        wait_alone(pool, load["wq"], 16 * i + 32, pool_waits)
                    wait_alone(pool, q_ps, NSTEP * i + NSTEP - G + h + 1, pool_waits)
                    split_in_loop(wq_h[:, :, h * HD:(h + 1) * HD], wq_l[:, :, h * HD:(h + 1) * HD],
                                  wq_r[:, :, h * HD:(h + 1) * HD], wq_split, 8 * i + len(WO_LATE) + 1 + h)
                if k in WO_EARLY:
                    h = WO_EARLY.index(k)
                    if h == 0:
                        wait_alone(pool, load["wo"], 16 * i + 32, pool_waits)
                    wait_alone(pool, wo_used, NSTEP * i + NSTEP - G + h + 1, pool_waits)
                    split_in_loop(wo_h[:, h, :], wo_l[:, h, :], wo_r[:, h, :], wo_split, 8 * i + len(WO_LATE) + 1 + G + h)

            def expert_preparations(n):
                if n < 2:
                    if n == 0:
                        pool.wait_ge(load["shared"], 48)
                    split(sgu_h[:, n, :, :], sgu_l[:, n, :, :], sgu_r[:, n, :, :], shared_split)
                elif n == 2:
                    split(sd_h[:, :, :], sd_l[:, :, :], sd_r[:, :, :], shared_split)
                else:
                    if n == 3:
                        pool.wait_ge(load["moe"], 16 * (2 * ND + 1))
                    split_group_part(0, 0, n - 3)

            def split_group_part(g, slot, n):
                if n < 2 * ND:
                    w, t = (wg_h, wg_l, wg_r) if n < ND else (wu_h, wu_l, wu_r), n % ND
                    h, l, r = w[0][:, slot, t, :], w[1][:, slot, t, :], w[2][:, t, :]
                else:
                    part = slice(0, 2) if n == 2 * ND else slice(2, JT)
                    h, l, r = wd_h[:, slot, part, :], wd_l[:, slot, part, :], wd_r[:, part, :]
                pool.tensor_copy(h, r).then_inc(moe_chain, 1)
                pool.wait_ge(moe_chain, g * 6 + n + 1)
                pool.tensor_tensor(l, r, h.bitcast(F32), ALU.subtract).then_inc(moe_split, 1)

            norm_scale(2, 1)
            attention(0, 2 - KV_LEAD, False)
            attention(0, 3 - KV_LEAD, False)
            for c in range(2, NPAIR):
                norm_scale(2, c)
            run_attention(pool, attention)
            norm_scale(3, NPAIR - 1)
            for n in range(len(PREPARE), 3 + 6):
                expert_preparations(n)

            def split_group(g, slot):
                wait_alone(pool, load["moe"], (g + 1) * 16 * (2 * ND + 1), pool_waits)
                wait_alone(pool, e_down, (g - 1) * UPG + NS * NHALF, pool_waits)
                for n in range(6):
                    split_group_part(g, slot, n)

            split_group(1, 1)
            with pool.Fori(1, NG // 2) as i:
                split_group(2 * i, 0)
                split_group(2 * i + 1, 1)

        @block.tensor
        def _(pe):
            def norm_transposes(m, c):
                pe.wait_ge(xn_ready, m * NPAIR + c + 1)
                for d in range(ND):
                    for t in range(2):
                        last = pe.transpose(ps[:, XT_BANKS[m][c], (2 * d + t) * P:(2 * d + t + 1) * P],
                                            xn[:, 2 * c + t, d * P:(d + 1) * P], ident[:, :])
                last.then_inc(xT_ps, 1)

            def keep_warm(n, bank):
                for _ in range(n):
                    pe.matmul(ps[:, bank, :].rearrange("p (a b) -> p a b", b=P), identb[:, :],
                              identb[:, :].unsqueeze(1).broadcast_to([P, 512 // P, P]), start=True, stop=True)

            pe.wait_ge(consts_made, 1)
            keep_warm(14, 7)
            for n in range(NHALF):
                for c in range(2 * n, 2 * n + 2):
                    norm_transposes(0, c)
                pe.wait_ge(load[f"ctx{n}"], 16)
                for d in range(ND):
                    for t in range(NT // 2):
                        last = pe.transpose(ps[:, 4 + ND * n + d, t * P:(t + 1) * P],
                                            ctx_sb[:, n * NT // 2 + t, d * P:(d + 1) * P], ident[:, :])
                    last.then_inc(ctxT_ps, 1)
            pe.wait_ge(ctxT_lo, ND)
            pe.wait_ge(xT_lo, NPAIR)

            units = NE0 * ND * NHALF

            def up(u):
                e, f, n = u // (ND * NHALF), u // NHALF % ND, u % NHALF
                if u >= 4:
                    pe.wait_ge(gated, u - 3)
                if u == WSS_UNIT + 1:
                    pe.wait_ge(wme_ready, 1)
                    pe.wait_ge(small_ready, 1)
                col = slice(e * D + f * P, e * D + (f + 1) * P)
                for d in range(ND):
                    last = three(pe, ps[:, u % 4, :], ctxT_h[:, d, col], ctxT_l[:, d, col],
                                 xT_h[:, d, n * HALF:(n + 1) * HALF], xT_l[:, d, n * HALF:(n + 1) * HALF],
                                 d == 0, d == ND - 1)
                last.then_inc(up_done, 1)

            def down(u):
                e, f, n = u // (ND * NHALF), u // NHALF % ND, u % NHALF
                pe.wait_ge(m_lo, u + 1)
                if u == 1:
                    pe.wait_ge(ctxT_lo, CTX_UNITS)
                for t in range(NT // 2):
                    tile = n * NT // 2 + t
                    last = three(pe, ps[:, 4 + tile // 2, tile % 2 * D:(tile % 2 + 1) * D],
                                 m_h[:, u % 3, t * P:(t + 1) * P], m_l[:, u % 3, t * P:(t + 1) * P],
                                 ctxT_h[:, f, e * D:(e + 1) * D], ctxT_l[:, f, e * D:(e + 1) * D],
                                 e == 0 and f == 0 and tile % 2 == 0, e == NE0 - 1 and f == ND - 1,
                                 skip_group_check=True)
                last.then_inc(down_done, 1)

            for u in range(units + M_LAG):
                if u < units:
                    up(u)
                if u == WSS_UNIT:
                    pe.wait_ge(gated, WSS_UNIT - 2)
                    pe.wait_ge(wss_ready, 2)
                    pe.wait_ge(load["small"], 48)
                    pe.transpose(ps[:, WSS_BANK, P:P + NH + 2], smalls[:, :], ident[0:NH + 2, 0:NH + 2])
                    pe.matmul(ps[:, WSS_BANK, 0:2], ones[:, :], wss[:, :], start=True, stop=True).then_inc(wss_ps, 1)
                if u >= M_LAG:
                    down(u - M_LAG)

            pe.wait_ge(w_round, 6)
            for d in range(ND):
                for f in range(NF):
                    last = pe.transpose(psb[:, d, f * P:(f + 1) * P], w1_q[:, f, d * P:(d + 1) * P], identb[:, :])
                last.then_inc(wT_ps, 1)
            pe.wait_ge(w_round, 12)
            for h in range(2):
                for f in range(NF // 2):
                    for d in range(ND):
                        last = pe.transpose(psb[:, 2 + h, f * D + d * P:f * D + (d + 1) * P],
                                            w2_q[:, d, (h * NF // 2 + f) * P:(h * NF // 2 + f + 1) * P], identb[:, :])
                last.then_inc(wT_ps, 1)
            def quantised_transposes(c):
                pe.wait_ge(xq_ready, c + 1)
                for d in range(ND):
                    for t in range(2):
                        last = pe.transpose(psb[:, 4 + c, (2 * d + t) * P:(2 * d + t + 1) * P],
                                            xq[:, 2 * c + t, d * P:(d + 1) * P], identb[:, :])
                last.then_inc(xqT_ps, 1)

            def ffn_up(t):
                pe.wait_ge(xqT_ready, t // 2 + 1)
                if t >= 2:
                    pe.wait_ge(h_ready, t - 1)
                for h in range(2):
                    for d in range(ND):
                        last = pe.matmul(ps[:, 2 * (t % 2) + h, :], xqT[:, d, t * P:(t + 1) * P],
                                         w1T[:, d, h * 512:(h + 1) * 512], start=(d == 0), stop=(d == ND - 1))
                last.then_inc(h_ps, 1)

            def ffn_transpose(t):
                pe.wait_ge(hq_ready, t + 1)
                if t >= 2:
                    pe.wait_ge(hT_ready, t - 1)
                for f in range(NF):
                    last = pe.transpose(psb[:, 4 + t % 2, f * P:(f + 1) * P], h_q[:, t % 2, f * P:(f + 1) * P], identb[:, :])
                last.then_inc(hT_ps, 1)

            def ffn_down(t):
                pe.wait_ge(hT_ready, t + 1)
                if t >= 2:
                    pe.wait_ge(x2_ready, t - 1)
                for f in range(NF):
                    last = pe.matmul(ps[:, 6 + t % 2, 0:D], hT[:, t % 2, f, :], w2T[:, f, :], start=(f == 0), stop=(f == NF - 1))
                last.then_inc(y_ps, 1)

            def attention(i, k, last_turn):
                g = NSTEP * i

                def live(j):
                    return j >= 0 and not (last_turn and j >= NSTEP)

                if 0 <= k < NPAIR:
                    pe.wait_ge(xT_lo, NPAIR + k + 1)

                if last_turn and k > NSTEP + LAG_Q:
                    if k == NSTEP + LAG_Q + 1:
                        pe.wait_ge(q_ve_ready, NSTEP * NKV)
                    keep_warm(4, 0)

                j = k - LAG_T
                if live(j):
                    pe.wait_ge(s_normed, 2 * (g + j) + 2)
                    if j >= 2:
                        pe.wait_ge(pT_lo, g + j - 1)
                    for kt in range(2):
                        for t in range(2):
                            last = pe.transpose(ps[:, 4 + j % 2, kt * S + t * P:kt * S + (t + 1) * P],
                                                sc[:, j % 4, t, kt * P:(kt + 1) * P], ident[:, :])
                    last.then_inc(pT_ps, 1)
                j = k - LAG_PV
                if live(j):
                    b = j // G % B
                    pe.wait_ge(pT_lo, g + j + 1)
                    if j % G == 0:
                        pe.wait_ge(v_lo, B * i + j // G + 1)
                    if j >= 1:
                        pe.wait_ge(o_lo, g + j)
                    for kt in range(2):
                        last = three(pe, ps[:, 6, 0:S], v_h[:, b, kt, :], v_l[:, b, kt, :], pT_h[:, j % 2, kt, :],
                                     pT_l[:, j % 2, kt, :], kt == 0, kt == 1)
                    last.then_inc(o_ps, 1)
                j = k - LAG_WO
                if live(j):
                    h = j % G
                    if j < G:
                        pe.wait_ge(wo_split, G * i + h + 1)
                    pe.wait_ge(o_lo, g + j + 1)
                    if h == 0:
                        pe.wait_ge(y_added, B * i + j // G + 1)
                    for t in range(2):
                        last = three(pe, ps[:, 7, t * D:(t + 1) * D], oT_h[:, j % 2, t * P:(t + 1) * P],
                                     oT_l[:, j % 2, t * P:(t + 1) * P], wo_h[:, h, :], wo_l[:, h, :],
                                     h == 0 and t == 0, h == G - 1, skip_group_check=True)
                    last.then_inc(wo_used, 1)
                j = k - LAG_Q
                if live(j):
                    if LAG_Q <= k < LAG_T:
                        keep_warm(4, 5)
                    pe.wait_ge(q_squared, g + j + 1)
                    pe.wait_ge(q_lo, g + j + 1)
                    for t in range(2):
                        last = pe.matmul(ps[:, 0, S + t:S + t + 1], q_sq[:, t * P:(t + 1) * P], ones[:, 0:1], start=True, stop=True)
                    last.then_inc(q_ss, 1)
                j = k - LAG_S
                if live(j):
                    if j >= 2:
                        pe.wait_ge(s_scaled, g + j - 1)
                    b = j // G % B
                    if j % G == 0:
                        pe.wait_ge(kT_lo, B * i + j // G + 1)
                    for t in range(2):
                        last = three(pe, ps[:, 2 + j % 2, t * S:(t + 1) * S], q_h[:, j % 2, t * P:(t + 1) * P],
                                     q_l[:, j % 2, t * P:(t + 1) * P], kT_h[:, b, :], kT_l[:, b, :], True, True)
                    last.then_inc(s_ps, 1)
                j = k
                if live(j):
                    b, h = j // G % B, j % G
                    if j % G == j:
                        pe.wait_ge(wq_split, G * i + h + 1)
                    elif j >= NSTEP:
                        pe.wait_ge(wq_split, G * i + G + h + 1)
                    if j >= 1:
                        pe.wait_ge(q_ve_ready, g + j)
                    for d in range(ND):
                        last = three(pe, ps[:, 0, 0:S], wq_h[:, d, h * HD:(h + 1) * HD], wq_l[:, d, h * HD:(h + 1) * HD],
                                     xT_h[:, d, b * S:(b + 1) * S], xT_l[:, d, b * S:(b + 1) * S], d == 0, d == ND - 1)
                    last.then_inc(q_ps, 1)
                b = kv_batch(k - 3)
                if b is not None and not (last_turn and b >= B):
                    pe.wait_ge(k_normed, B * i + b + 1)
                    for t in range(2):
                        last = pe.transpose(ps[:, 1, t * P:(t + 1) * P], k_n[:, t, :], ident[:, :])
                    last.then_inc(kT_ps, 1)
                b = kv_batch(k)
                if b is not None and not (last_turn and b >= B):
                    c = B * i + b
                    pe.wait_ge(kv_split, i + b // B + 1)
                    if not (k < FIRST and b == 0):
                        pe.wait_ge(kT_lo, c)
                    tok = (b % B) * S
                    for t in range(2):
                        for d in range(ND):
                            last = three(pe, ps[:, 1, t * 2 * HD:(t + 1) * 2 * HD],
                                         ctxT_h[:, d, tok + t * P:tok + (t + 1) * P], ctxT_l[:, d, tok + t * P:tok + (t + 1) * P],
                                         wkv_h[:, d, :], wkv_l[:, d, :], d == 0, d == ND - 1)
                    last.then_inc(kv_ps, 1)
                c = added_batch(k - 3)
                if last_turn and c is not None:
                    if c == 0:
                        pe.wait_ge(kT_lo, B * NKV)
                    else:
                        pe.wait_ge(xT_lo, 2 * NPAIR + c)
                    norm_transposes(2, c)
                if last_turn and k in GATE_STEPS:
                    gate(GATE_STEPS.index(k))

            def gate(c):
                pe.wait_ge(xT_lo, 2 * NPAIR + c + 1)
                if c == 0:
                    pe.wait_ge(gw_split, 1)
                    pe.wait_ge(s_scaled, NSTEP * NKV - 1)
                for t in range(2 * c, 2 * c + 2):
                    for d in range(ND):
                        last = three(pe, ps[:, 2, t * NE:(t + 1) * NE], xT_h[:, d, t * P:(t + 1) * P],
                                     xT_l[:, d, t * P:(t + 1) * P], gw_h[:, d, :], gw_l[:, d, :], d == 0, d == ND - 1)
                last.then_inc(gate_ps, 1)

            pe.wait_ge(wT_ready, 4)
            keep_warm(12, 0)
            quantised_transposes(0)
            ffn_up(0)
            quantised_transposes(1)
            ffn_up(1)
            quantised_transposes(2)
            ffn_up(2)
            quantised_transposes(3)
            ffn_up(3)
            for t in range(NT):
                if t + H_LEAD < NT:
                    ffn_up(t + H_LEAD)
                ffn_transpose(t)
                if t >= 1:
                    ffn_down(t - 1)
                if t == NT - 3:
                    pe.wait_ge(h_ready, NT)
                    attention(0, -KV_LEAD, False)

            ffn_down(NT - 1)
            attention(0, 3 - KV_LEAD, False)
            attention(0, 4 - KV_LEAD, False)
            for c in range(NPAIR):
                norm_transposes(1, c)
            run_attention(pe, attention)


            def shared_up(u):
                f, n = u // NHALF, u % NHALF
                tok = slice(n * HALF, (n + 1) * HALF)
                if u == 0:
                    pe.wait_ge(xT_lo, 2 * NPAIR + 3)
                if u == 1:
                    pe.wait_ge(gate_sig, 1)
                if u >= 2:
                    pe.wait_ge(e_comb, u - 1)
                for m, done in ((0, eg_ps), (1, eu_ps)):
                    for d in range(ND):
                        last = three(pe, ps[0:FSH, 2 * (u % 2) + m, :], sgu_h[:, m, d, f * FSH:(f + 1) * FSH],
                                     sgu_l[:, m, d, f * FSH:(f + 1) * FSH], xT_h[:, d, tok], xT_l[:, d, tok], d == 0, d == ND - 1)
                    last.then_inc(done, 1)

            def shared_down(u):
                f, n = u // NHALF, u % NHALF
                pe.wait_ge(e_lo, u + 1)
                for d in range(ND):
                    last = three(pe, ps[:, 4 + ND * n + d, :], sd_h[:, f, d * P:(d + 1) * P], sd_l[:, f, d * P:(d + 1) * P],
                                 e_h[0:FSH, u % 3, :], e_l[0:FSH, u % 3, :], f == 0, False, skip_group_check=True)
                last.then_inc(e_down, 1)

            pe.wait_ge(shared_split, 3)
            SU = NS * NHALF
            shared_up(0)
            norm_transposes(2, NPAIR - 1)
            gate(NPAIR - 1)
            shared_up(1)
            shared_up(2)
            shared_down(0)
            pe.wait_ge(c_ready, 1)
            for t in range(NT):
                last = pe.transpose(ps[0:NE, 6 + t // (NT // 2), t % (NT // 2) * P:(t % (NT // 2) + 1) * P],
                                    gc[:, t, :], ident[:, :])
            last.then_inc(cT_ps, 1)
            shared_up(3)
            shared_down(2)
            pe.wait_ge(cT_ready, 1)
            shared_down(1)
            shared_down(3)

            def experts(i, k, last_turn):
                u0 = UNITS * i + SU
                if not (last_turn and k >= UNITS):
                    slot, f, n = k // UPG % 2, k % UPG // NHALF, k % NHALF
                    tok = slice(n * HALF, (n + 1) * HALF)
                    if k % UPG == 0:
                        pe.wait_ge(moe_split, 6 * (2 * i + k // UPG + 1))
                    pe.wait_ge(e_comb, u0 + k - 1)
                    for m, wh, wl, done in ((0, wg_h, wg_l, eg_ps), (1, wu_h, wu_l, eu_ps)):
                        for d in range(ND):
                            last = three(pe, ps[:, 2 * (k % 2) + m, :], wh[:, slot, d, f * P:(f + 1) * P],
                                         wl[:, slot, d, f * P:(f + 1) * P], xT_h[:, d, tok], xT_l[:, d, tok],
                                         d == 0, d == ND - 1)
                        last.then_inc(done, 1)
                j = k - LAG_DOWN
                if j >= 0:
                    slot, f, n = j // UPG % 2, j % UPG // NHALF, j % NHALF
                    pe.wait_ge(e_lo, u0 + j + 1)
                    for d in range(ND):
                        last = three(pe, ps[:, 4 + ND * n + d, :], wd_h[:, slot, f, d * P:(d + 1) * P],
                                     wd_l[:, slot, f, d * P:(d + 1) * P], e_h[:, j % 3, :], e_l[:, j % 3, :],
                                     False, last_turn and j >= UNITS - NHALF, skip_group_check=True)
                    last.then_inc(e_down, 1)

            run_experts(pe, experts)

            for n in range(NT // 2):
                pe.wait_ge(yT_ready, ND * (n // 2 + 1))
                for t in range(2):
                    for d in range(ND):
                        last = pe.transpose(ps[:, n, t * D + d * P:t * D + (d + 1) * P],
                                            yT[:, d, (2 * n + t) * P:(2 * n + t + 1) * P], ident[:, :])
                last.then_inc(yb_ps, 1)

        @block.scalar
        def _(act):
            act.wait_ge(consts_made, 1)
            act.activation(k_ss[:, :], neg_half[:, :], ACT.Silu)

            def norm_high(m, c):
                act.wait_ge(xT_ps, m * NPAIR + c + 1)
                act.activation(xT_h[:, :, 2 * c * P:2 * (c + 1) * P],
                               ps[:, XT_BANKS[m][c], :].rearrange("p (d t) -> p d t", d=ND), ACT.Copy).then_inc(xT_hi, 1)

            for n in range(NHALF):
                for c in range(2 * n, 2 * n + 2):
                    norm_high(0, c)
                for d in range(ND):
                    act.wait_ge(ctxT_ps, ND * n + d + 1)
                    act.activation(ctxT_h[:, d, n * HALF:(n + 1) * HALF], ps[:, 4 + ND * n + d, :], ACT.Copy).then_inc(ctxT_hi, 1)
            units = NE0 * ND * NHALF

            def m_high(u):
                act.wait_ge(masked, u + 1)
                if u >= 3:
                    act.wait_ge(down_done, u - 2)
                act.activation(m_h[:, u % 3, :], m_t[:, u % 2, :], ACT.Copy).then_inc(m_hi, 1)

            for u in range(units):
                act.wait_ge(up_done, u + 1)
                if u >= 2:
                    act.wait_ge(gated, u - 1)
                act.activation(m_s[:, u % 2, :], ps[:, u % 4, :], ACT.Silu).then_inc(silu_done, 1)
                if u == 1:
                    act.wait_ge(load["w1"], 16)
                    act.activation(w1_q[:, :, :], w1_sb[:, :, :], ACT.Square, accum_out=wss[:, 0:1]).then_inc(wss_ready, 1)
                if u == 3:
                    act.wait_ge(load["w2"], 16)
                    act.activation(w2_q[:, :, :], w2_sb[:, :, :], ACT.Square, accum_out=wss[:, 1:2]).then_inc(wss_ready, 1)
                if u == WSS_UNIT:
                    act.wait_ge(wme_ready, 1)
                    act.activation(bqT[:, :], ps[:, WSS_BANK, P:P + NH], ACT.Copy).then_inc(small_ready, 1)
                if u >= 1:
                    m_high(u - 1)
            m_high(units - 1)
            act.activation(k_ss[:, :], neg_half[:, :], ACT.Gelu)

            for c in range(2):
                act.wait_ge(wT_ps, c + 1)
                act.activation(w1T[:, c, :], psb[:, c, :], ACT.Copy).then_inc(wT_ready, 1)
            for c in range(2):
                act.wait_ge(wT_ps, c + 3)
                act.activation(w2T[:, c * NF // 2:(c + 1) * NF // 2, :].rearrange("p a b -> p (a b)"),
                               psb[:, 2 + c, :], ACT.Copy).then_inc(wT_ready, 1)

            def quantised(c):
                act.wait_ge(x_rounded, c + 1)
                act.activation(xq[:, 2 * c:2 * c + 2, :], xn[:, 2 * c:2 * c + 2, :], ACT.Identity,
                               bias=neg_magic[:, 0:1]).then_inc(x_integers, 1)

            def quantised_copy(c):
                act.wait_ge(xqT_ps, c + 1)
                act.activation(xqT[:, :, 2 * c * P:2 * (c + 1) * P],
                               psb[:, 4 + c, 0:2 * ND * P].rearrange("p (d t) -> p d t", d=ND), ACT.Copy).then_inc(xqT_ready, 1)

            def hidden(t):
                act.wait_ge(h_ps, t + 1)
                if t % 2 == 0:
                    act.wait_ge(act_scale_ready, t // 2 + 1)
                if t >= HS:
                    act.wait_ge(h_integers, t - HS + 1)
                act.activation(h_slots[t % HS], ps[:, 2 * (t % 2):2 * (t % 2) + 2, :].rearrange("p a b -> p (a b)"),
                               ACT.Gelu, scale=adeq[:, t:t + 1]).then_inc(h_ready, 1)

            def hT_copy(t):
                act.wait_ge(hT_ps, t + 1)
                if t >= 2:
                    act.wait_ge(y_ps, t - 1)
                act.activation(hT[:, t % 2, :, :].rearrange("p a b -> p (a b)"), psb[:, 4 + t % 2, :], ACT.Copy).then_inc(hT_ready, 1)

            def attention(i, k, last_turn):
                g = NSTEP * i

                def live(j):
                    return j >= 0 and not (last_turn and j >= NSTEP)

                j = k - LAG_Q
                if live(j):
                    if j >= 2:
                        wait_alone(act, s_ps, g + j - 1, act_waits)
                    wait_alone(act, q_ps, g + j + 1, act_waits)
                    head = G * i + j % G + G * (j // NSTEP)
                    act.activation(q_h[:, j % 2, :], ps[:, 0, 0:S], ACT.Identity, bias=bqT[:, bass.ds(head, 1)]).then_inc(q_hi, 1)
                    if j >= 1:
                        wait_alone(act, q_ss, g + j, act_waits)
                    act.activation(q_sq[:, :], ps[:, 0, 0:S], ACT.Square, bias=bqT[:, bass.ds(head, 1)]).then_inc(q_squared, 1)
                j = k - LAG_EXP
                if live(j):
                    act.wait_ge(s_max, g + j + 1)
                    for t in range(2):
                        last = act.activation(sc[:, j % 4, t, :], sc[:, j % 4, t, :], ACT.Exp, bias=nmax[:, j % 2, t:t + 1],
                                              accum_out=esum[:, j % 2, t:t + 1])
                    last.then_inc(s_exp, 1)
                b = kv_batch(k - 4)
                if b is not None and not (last_turn and b >= B):
                    act.wait_ge(kT_ps, B * i + b + 1)
                    act.activation(kT_h[:, b % B, :], ps[:, 1, 0:S], ACT.Copy).then_inc(kT_hi, 1)
                b = kv_batch(k - 2)
                if b is not None and not (last_turn and b >= B):
                    act.wait_ge(kv_biased, B * i + b + 1)
                    for t in range(2):
                        last = act.activation(k_sq[:, t, :], kv_sb[:, t, 0:HD], ACT.Square, accum_out=k_ss[:, t:t + 1])
                    last.then_inc(k_squared, 1)
                j = k - LAG_T
                if live(j):
                    act.wait_ge(pT_ps, g + j + 1)
                    if j >= 2:
                        act.wait_ge(o_ps, g + j - 1)
                    act.activation(pT_h[:, j % 2, :, :].rearrange("p a b -> p (a b)"), ps[:, 4 + j % 2, :], ACT.Copy).then_inc(pT_hi, 1)
                j = k - LAG_PV
                if live(j):
                    act.wait_ge(o_ps, g + j + 1)
                    act.activation(oT_h[:, j % 2, :], ps[:, 6, 0:S], ACT.Copy).then_inc(o_hi, 1)
                b = kv_batch(k - 2)
                if b is not None and not (last_turn and b >= B):
                    act.activation(v_h[:, b % B, :, :], kv_sb[:, :, HD:2 * HD], ACT.Copy).then_inc(v_hi, 1)
                if last_turn and added_batch(k - 3) is not None:
                    norm_high(2, added_batch(k - 3))
                if k == KV_SPLIT - 1 and not last_turn:
                    act.wait_ge(load["wkv"], 32 * i + 64)
                    act.wait_ge(kv_ps, B * i + B)
                    act.activation(wkv_h[:, :, :], wkv_r[:, :, :], ACT.Copy).then_inc(kv_hi, 1)

            for c in range(NPAIR):
                quantised(c)
                quantised_copy(c)
                if c >= 1:
                    hidden(c - 1)
            hidden(NPAIR - 1)
            for t in range(NT):
                if t + H_LEAD < NT:
                    hidden(t + H_LEAD)
                hT_copy(t)
                if t == NT - 3:
                    attention(0, 2 - KV_LEAD, False)

            attention(0, 4 - KV_LEAD, False)
            for c in range(NPAIR):
                norm_high(1, c)
            run_attention(act, attention)
            norm_high(2, NPAIR - 1)

            act.wait_ge(gate_ps, NPAIR)
            act.activation(gs[:, :, 0:NE], ps[:, 2, 0:NT * NE].rearrange("p (t e) -> p t e", e=NE), ACT.Sigmoid).then_inc(gate_sig, 1)

            SU = NS * NHALF
            for u in range(SU + 1):
                if u < SU:
                    act.wait_ge(eg_ps, u + 1)
                    if u >= 2:
                        act.wait_ge(e_lo, u - 1)
                    act.activation(e_s[0:FSH, u % 2, :], ps[0:FSH, 2 * (u % 2), :], ACT.Silu).then_inc(e_silu, 1)
                if u >= 1:
                    j = u - 1
                    act.wait_ge(e_comb, j + 1)
                    if j >= 3:
                        act.wait_ge(e_down, j - 2)
                    act.activation(e_h[0:FSH, j % 3, :], e_s[0:FSH, j % 2, :], ACT.Copy).then_inc(e_hi, 1)
                if u == SU - 2:
                    act.wait_ge(cT_ps, 1)
                    act.activation(cT[:, :], ps[0:NE, 6:8, :].rearrange("p a b -> p (a b)"), ACT.Copy).then_inc(cT_ready, 1)

            def experts(i, k, last_turn):
                u0 = UNITS * i + SU
                j = k - 1
                if j >= 0 and not (last_turn and j >= UNITS):
                    act.wait_ge(e_comb, u0 + j + 1)
                    act.wait_ge(e_down, u0 + j - 2)
                    act.activation(e_h[:, j % 3, :], e_s[:, j % 2, :], ACT.Copy).then_inc(e_hi, 1)
                if not (last_turn and k >= UNITS):
                    act.wait_ge(eg_ps, u0 + k + 1)
                    act.wait_ge(e_lo, u0 + k - 1)
                    act.activation(e_s[:, k % 2, :], ps[:, 2 * (k % 2), :], ACT.Silu).then_inc(e_silu, 1)

            run_experts(act, experts)
            for n in range(NHALF):
                act.wait_ge(e_down, NG * UPG + SU - 1 + n)
                for d in range(ND):
                    act.activation(yT[:, d, n * HALF:(n + 1) * HALF], ps[:, 4 + ND * n + d, :], ACT.Copy).then_inc(yT_ready, 1)


        @block.vector
        def _(dve):
            step = [0]

            def mark(ins):
                step[0] += 1
                ins.then_inc(dve_step, 1)
                return step[0]

            def after(n):
                dve.wait_ge(dve_step, n)

            def link(ins):
                after(mark(ins))

            def stats(t):
                return dve.bn_stats(stat6[:, t, :], x_sb[:, t, :])

            def mean_variance(t):
                return dve.bn_aggr(mv[:, t, :], stat6[:, t, :])

            def variance_eps(c):
                dve.tensor_scalar(veps[:, 2 * c:2 * c + 2], mv[:, 2 * c:2 * c + 2, 1], LN_EPS, None, ALU.add).then_inc(stat_ready, 1)

            def pair_stats(c):
                stats(2 * c)
                link(stats(2 * c + 1))
                mean_variance(2 * c)
                link(mean_variance(2 * c + 1))
                variance_eps(c)

            def norm(n, c):
                dve.wait_ge(rstd_ready, n * NPAIR + c + 1)
                for t in range(2 * c, 2 * c + 2):
                    last = dve.tensor_scalar(xn[:, t, :], x_sb[:, t, :], mv[:, t, 0:1], rstd[:, t:t + 1],
                                             ALU.subtract, ALU.mult)
                return last

            def last_added(b):
                dve.wait_ge(y_added, B * (NKV - 1) + b + 2)
                pair_stats(b)

            def norm_low(m, c):
                dve.wait_ge(xT_hi, m * NPAIR + c + 1)
                tok = slice(2 * c * P, 2 * (c + 1) * P)
                dve.tensor_tensor(xT_l[:, :, tok], ps[:, XT_BANKS[m][c], :].rearrange("p (d t) -> p d t", d=ND),
                                  xT_h[:, :, tok].bitcast(F32), ALU.subtract).then_inc(xT_lo, 1)

            for c in range(NPAIR):
                if c % 2 == 0:
                    dve.wait_ge(load[f"x{c // 2}"], 16)
                pair_stats(c)
            for c in range(NPAIR):
                norm(0, c).then_inc(xn_ready, 1)

            def expert_mask(e):
                if e == 0:
                    dve.wait_ge(load["itok"], 16)
                    ins = dve.tensor_scalar(emask[:, e, :], itok_sb[:, :], float(SPAN), None, ALU.is_lt)
                elif e == NE0 - 1:
                    ins = dve.tensor_scalar(emask[:, e, :], itok_sb[:, :], float(SPAN * e), None, ALU.is_ge)
                else:
                    dve.wait_ge(emask_made, e)
                    link(dve.tensor_scalar(above, itok_sb[:, :], float(SPAN * (e + 1)), None, ALU.is_ge))
                    ins = dve.scalar_tensor_tensor(out=emask[:, e, :], in0=itok_sb[:, :], scalar=float(SPAN * e),
                                                   in1=above, op0=ALU.is_ge, op1=ALU.subtract)
                ins.then_inc(emask_made, 1)

            def ctx_low(c):
                n, d = c // ND, c % ND
                tok = slice(n * HALF, (n + 1) * HALF)
                dve.wait_ge(ctxT_hi, c + 1)
                dve.tensor_tensor(ctxT_l[:, d, tok], ps[:, 4 + c, :], ctxT_h[:, d, tok].bitcast(F32),
                                  ALU.subtract).then_inc(ctxT_lo, 1)

            for c in range(2):
                norm_low(0, c)
            for c in range(ND):
                ctx_low(c)
            for c in range(2, NPAIR):
                norm_low(0, c)
            expert_mask(0)

            above = sc[:, 2:4, :, :].rearrange("p a b c -> p (a b c)")
            w1f = w1_sb[:, :, :].rearrange("p a b -> p (a b)")
            w2f = w2_sb[:, :, :].rearrange("p a b -> p (a b)")
            w1qf = w1_q[:, :, :].rearrange("p a b -> p (a b)")
            w2qf = w2_q[:, :, :].rearrange("p a b -> p (a b)")

            def quantise_weights(n):
                m, op, h = n // 6, n // 2 % 3, n % 2
                w, q = ((w1f, w1qf), (w2f, w2qf))[m]
                c = slice(h * FF, (h + 1) * FF)
                if n == 0:
                    dve.wait_ge(wrms_ready, 1)
                if n >= 2:
                    dve.wait_ge(w_round, n - 1)
                if op == 0:
                    last = dve.tensor_scalar(w[:, c], w[:, c], wrms[:, m:m + 1], 1.0, ALU.mult, ALU.min)
                elif op == 1:
                    last = dve.tensor_scalar(w[:, c], w[:, c], -1.0, MAGIC, ALU.max, ALU.add)
                else:
                    last = dve.tensor_scalar(q[:, c], w[:, c], -MAGIC, None, ALU.add)
                last.then_inc(w_round, 1)

            units = NE0 * ND * NHALF

            def gate_unit(u):
                dve.wait_ge(silu_done, u + 1)
                if u >= 2:
                    dve.wait_ge(m_lo, u - 1)
                dve.tensor_tensor(m_t[:, u % 2, :], m_s[:, u % 2, :], ps[:, u % 4, :], ALU.mult).then_inc(gated, 1)

            def low_unit(u):
                dve.wait_ge(m_hi, u + 1)
                dve.tensor_tensor(m_l[:, u % 3, :], m_t[:, u % 2, :], m_h[:, u % 3, :].bitcast(F32),
                                  ALU.subtract).then_inc(m_lo, 1)

            quantised = 0
            for u in range(units):
                gate_unit(u)
                if u == WSS_UNIT:
                    dve.wait_ge(wss_ps, 1)
                    dve.tensor_scalar(wme[:, :], ps[:, WSS_BANK, 0:2], 1.0 / (FF * D), Q_EPS, ALU.mult, ALU.max).then_inc(wme_ready, 1)
                if u >= 1:
                    low_unit(u - 1)
                if u == 0:
                    for c in range(ND, CTX_UNITS):
                        ctx_low(c)
                elif u in (2, 5, 8):
                    expert_mask(u // 3 + 1)
                elif u > WSS_UNIT:
                    quantise_weights(quantised)
                    quantised += 1
                    if u >= units - 3:
                        quantise_weights(quantised)
                        quantised += 1
            low_unit(units - 1)
            for c in range(NPAIR + 2):
                if c < NPAIR:
                    pair = x_sb[:, 2 * c:2 * c + 2, :].rearrange("p a b -> p (a b)")
                    dve.wait_ge(down_done, units - 1 + c // 2)
                    added = mark(dve.tensor_tensor(pair, pair, ps[:, 4 + c, :], ALU.add))
                if 1 <= c <= NPAIR:
                    p = slice(2 * c - 2, 2 * c)
                    normed = mark(norm(1, c - 1))
                if c < NPAIR:
                    after(added)
                    stats(2 * c)
                    summed = mark(stats(2 * c + 1))
                if 1 <= c <= NPAIR:
                    after(normed)
                    largest = mark(dve.tensor_reduce(amax[:, p], xn[:, p, :], AX.X, ALU.max, apply_absolute_value=True))
                if c < NPAIR:
                    after(summed)
                    mean_variance(2 * c)
                    aggregated = mark(mean_variance(2 * c + 1))
                if 1 <= c <= NPAIR:
                    after(largest)
                    unit = mark(dve.tensor_scalar(amax[:, p], amax[:, p], Q_EPS, 1.0 / 127.0, ALU.max, ALU.mult))
                if c < NPAIR:
                    after(aggregated)
                    variance_eps(c)
                if 1 <= c <= NPAIR:
                    after(unit)
                    dve.reciprocal(ascl[:, p], amax[:, p]).then_inc(x_scale_ready, 1)
                    dve.tensor_scalar(adeq[:, p], amax[:, p], wirms[:, 0:1], None, ALU.mult).then_inc(act_scale_ready, 1)
                if c >= 2:
                    dve.wait_ge(x_integers, c - 1)
                    p = slice(2 * c - 4, 2 * c - 2)
                    dve.tensor_scalar(xq[:, p, :], xq[:, p, :], -128.0, 127.0, ALU.max, ALU.min).then_inc(xq_ready, 1)

            def attention(i, k, last_turn):
                g = NSTEP * i

                def live(j):
                    return j >= 0 and not (last_turn and j >= NSTEP)

                if last_turn and added_batch(k - 4) is not None:
                    norm_low(2, added_batch(k - 4))

                j = k - LAG_MAX
                if live(j):
                    dve.wait_ge(s_ps, g + j + 1)
                    dve.wait_ge(q_rs_ready, g + j + 1)
                    if j >= 4:
                        dve.wait_ge(pT_ps, g + j - 3)
                    for t in range(2):
                        last = dve.scalar_tensor_tensor(out=sc[:, j % 4, t, :], in0=ps[:, 2 + j % 2, t * S:(t + 1) * S],
                                                        scalar=q_rs[:, j % 2, t:t + 1], in1=mask_sb[:, t, :],
                                                        op0=ALU.mult, op1=ALU.add)
                    last.then_inc(s_scaled, 1)
                j = k - LAG_Q
                if live(j):
                    head = G * i + j % G + G * (j // NSTEP)
                    dve.wait_ge(q_squared, g + j + 1)
                    dve.scalar_tensor_tensor(out=q_l[:, j % 2, :], in0=ps[:, 0, 0:S], scalar=bqT[:, bass.ds(head, 1)],
                                             in1=q_h[:, j % 2, :].bitcast(F32), op0=ALU.add, op1=ALU.subtract).then_inc(q_lo, 1)
                j = k - LAG_MAX
                if live(j):
                    dve.wait_ge(s_scaled, g + j + 1)
                    dve.tensor_reduce(nmax[:, j % 2, :], sc[:, j % 4, :, :], AX.X, ALU.max, negate=True).then_inc(s_max, 1)
                j = k - LAG_EXP
                if live(j):
                    dve.wait_ge(s_exp, g + j + 1)
                    dve.reciprocal(einv[:, j % 2, :], esum[:, j % 2, :]).then_inc(s_inv, 1)
                j = k - LAG_Q
                if live(j):
                    dve.wait_ge(q_ss, g + j + 1)
                    dve.tensor_scalar(q_ve[:, j % 2, :], ps[:, 0, S:S + 2], HD * RMS_EPS, None, ALU.add).then_inc(q_ve_ready, 1)
                b = kv_batch(k - 4)
                if b is not None and not (last_turn and b >= B):
                    c = B * i + b
                    dve.wait_ge(kT_hi, c + 1)
                    dve.tensor_tensor(kT_l[:, b % B, :], ps[:, 1, 0:S], kT_h[:, b % B, :].bitcast(F32), ALU.subtract).then_inc(kT_lo, 1)
                b = kv_batch(k - 3)
                if b is not None and not (last_turn and b >= B):
                    c = B * i + b
                    dve.wait_ge(k_rs_ready, c + 1)
                    if k > 3 - KV_LEAD:
                        dve.wait_ge(kT_ps, c)
                    for t in range(2):
                        last = dve.scalar_tensor_tensor(out=k_n[:, t, :], in0=kv_sb[:, t, 0:HD], scalar=k_rs[:, t:t + 1],
                                                        in1=knq[:, :], op0=ALU.mult, op1=ALU.mult)
                    last.then_inc(k_normed, 1)
                b = kv_batch(k - 2)
                if b is not None and not (last_turn and b >= B):
                    dve.wait_ge(k_squared, B * i + b + 1)
                    dve.tensor_scalar(k_ve[:, :], k_ss[:, :], 1.0 / HD, RMS_EPS, ALU.mult, ALU.add).then_inc(k_ve_ready, 1)
                j = k - LAG_T
                if live(j):
                    dve.wait_ge(pT_hi, g + j + 1)
                    dve.tensor_tensor(pT_l[:, j % 2, :, :].rearrange("p a b -> p (a b)"), ps[:, 4 + j % 2, :],
                                      pT_h[:, j % 2, :, :].rearrange("p a b -> p (a b)").bitcast(F32), ALU.subtract).then_inc(pT_lo, 1)
                j = k - LAG_PV
                if live(j):
                    dve.wait_ge(o_hi, g + j + 1)
                    dve.tensor_tensor(oT_l[:, j % 2, :], ps[:, 6, 0:S], oT_h[:, j % 2, :].bitcast(F32), ALU.subtract).then_inc(o_lo, 1)
                b = kv_batch(k - 1)
                if b is not None and not (last_turn and b >= B):
                    c = B * i + b
                    dve.wait_ge(kv_ps, c + 1)
                    if k > 1 - KV_LEAD:
                        dve.wait_ge(v_lo, c)
                    for t in range(2):
                        last = dve.tensor_tensor(kv_sb[:, t, :].rearrange("p (a h) -> p a h", a=2),
                                                 ps[:, 1, t * 2 * HD:(t + 1) * 2 * HD].rearrange("p (a h) -> p a h", a=2),
                                                 bkv[:, :, bass.ds((i + b // B) * HD, HD)], ALU.add)
                    last.then_inc(kv_biased, 1)
                j = k - LAG_WO
                if live(j) and j % G == G - 1:
                    b = j // G
                    dve.wait_ge(wo_used, g + j + 1)
                    xb = x_sb[:, 2 * b:2 * b + 2, :].rearrange("p a b -> p (a b)")
                    dve.tensor_tensor(xb, xb, ps[:, 7, :], ALU.add).then_inc(y_added, 1)
                if last_turn and added_batch(k - 1) is not None:
                    last_added(added_batch(k - 1))
                if last_turn and added_batch(k - 2) is not None:
                    norm(3, added_batch(k - 2)).then_inc(xn_ready, 1)

            for t in range(NT + 5):
                j = t - H_LAG
                if 0 <= j < NT:
                    dve.wait_ge(h_integers, j + 1)
                    dve.tensor_scalar(h_q[:, j % 2, :], h_q[:, j % 2, :], -128.0, 127.0, ALU.max, ALU.min).then_inc(hq_ready, 1)
                if t < NT:
                    one = slice(t, t + 1)
                    dve.wait_ge(h_ready, t + 1)
                    largest = mark(dve.tensor_reduce(hmax[:, one], h_slots[t % HS], AX.X, ALU.max, apply_absolute_value=True))
                if t < NT:
                    after(largest)
                    unit = mark(dve.tensor_scalar(hmax[:, one], hmax[:, one], Q_EPS, 1.0 / 127.0, ALU.max, ALU.mult))
                j = t - 5
                if 0 <= j < NT:
                    dve.wait_ge(x2_ready, j + 1)
                    summed = mark(stats(j))
                if t < NT:
                    after(unit)
                    dve.reciprocal(hscl[:, one], hmax[:, one]).then_inc(h_scale_ready, 1)
                    dve.tensor_scalar(hdeq[:, one], hmax[:, one], wirms[:, 1:2], None, ALU.mult)
                j = t - 4
                if 0 <= j < NT:
                    dve.wait_ge(y_ps, j + 1)
                    dve.scalar_tensor_tensor(out=x_sb[:, j, :], in0=ps[:, 6 + j % 2, 0:D], scalar=hdeq[:, j:j + 1],
                                             in1=x_sb[:, j, :], op0=ALU.mult, op1=ALU.add).then_inc(x2_ready, 1)
                j = t - 5
                if 0 <= j < NT:
                    after(summed)
                    aggregated = mark(mean_variance(j))
                    if j % 2 == 1:
                        after(aggregated)
                        variance_eps(j // 2)
                if t in (NT, NT + 1):
                    norm(2, t - NT).then_inc(xn_ready, 1)
                if t == NT - 1:
                    dve.wait_ge(load["bkv"], 32)
                    attention(0, 1 - KV_LEAD, False)
                if t == NT:
                    attention(0, 2 - KV_LEAD, False)
                if t == NT + 1:
                    dve.wait_ge(knq_made, 1)
                    attention(0, 3 - KV_LEAD, False)
                if t == NT + 3:
                    attention(0, 4 - KV_LEAD, False)
            dve.wait_ge(load["mask"], 16)
            dve.memset(nmax[:, :, :], 0.0).then_inc(y_added, 1)
            norm(2, 2).then_inc(xn_ready, 1)
            norm(2, 3).then_inc(xn_ready, 1)
            for c in range(NPAIR):
                norm_low(1, c)

            run_attention(dve, attention)

            last_added(NPAIR - 1)
            norm(3, NPAIR - 1).then_inc(xn_ready, 1)
            norm_low(2, NPAIR - 1)
            dve.memset(gs[:, :, NE:NE + 2], -1.0)

            def combine_weights(n):
                if n == 0:
                    dve.wait_ge(gate_sig, 1)
                    for t in range(NT):
                        last = dve.max(gtop[:, t, :], gs[:, t, 0:NE])
                    link(last)
                    link(dve.tensor_reduce(gsum[:, :], gtop[:, :, 0:TOPK], AX.X, ALU.add))
                    link(dve.memset(gtop[:, :, TOPK:8], -1.0))
                else:
                    for t in range(NT):
                        last = dve.match_replace(out=grep[:, t, :], in_to_replace=gtop[:, t, :], in_values=gs[:, t, :],
                                                 imm_value=0.0)
                    link(dve.tensor_scalar(gsum[:, :], gsum[:, :], 1e-20, None, ALU.add))
                    link(dve.reciprocal(grec[:, :], gsum[:, :]))
                    link(dve.tensor_tensor(gc[:, :, :], gs[:, :, 0:NE], grep[:, :, 0:NE], ALU.subtract))
                    dve.tensor_tensor(gc[:, :, :], gc[:, :, :], grec[:, :].unsqueeze(2).broadcast_to([P, NT, NE]),
                                      ALU.mult).then_inc(c_ready, 1)

            SU = NS * NHALF
            for u in range(SU + 1):
                if u >= 1:
                    j = u - 1
                    dve.wait_ge(e_hi, j + 1)
                    dve.tensor_tensor(e_l[0:FSH, j % 3, :], e_s[0:FSH, j % 2, :], e_h[0:FSH, j % 3, :].bitcast(F32),
                                      ALU.subtract).then_inc(e_lo, 1)
                if u < SU:
                    dve.wait_ge(e_silu, u + 1)
                    dve.wait_ge(eu_ps, u + 1)
                    dve.tensor_tensor(e_s[0:FSH, u % 2, :], e_s[0:FSH, u % 2, :], ps[0:FSH, 2 * (u % 2) + 1, :],
                                      ALU.mult).then_inc(e_comb, 1)
                if u < 2:
                    combine_weights(u)

            def experts(i, k, last_turn):
                u0 = UNITS * i + SU
                j = k - 1
                if j >= 0 and not (last_turn and j >= UNITS):
                    dve.wait_ge(e_hi, u0 + j + 1)
                    dve.tensor_tensor(e_l[:, j % 3, :], e_s[:, j % 2, :], e_h[:, j % 3, :].bitcast(F32), ALU.subtract).then_inc(e_lo, 1)
                if not (last_turn and k >= UNITS):
                    dve.wait_ge(e_silu, u0 + k + 1)
                    dve.wait_ge(eu_ps, u0 + k + 1)
                    dve.tensor_tensor(e_s[:, k % 2, :], e_s[:, k % 2, :], ps[:, 2 * (k % 2) + 1, :], ALU.mult).then_inc(e_mult, 1)
                    dve.wait_ge(e_mult, UNITS * i + k + 1)
                    slot, f, n = k // UPG % 2, k % UPG // NHALF, k % NHALF
                    if k % UPG == 0:
                        dve.wait_ge(load[f"comb{slot}"], 16 * COMB_DMAS * (i + k // UNITS + 1))
                    dve.tensor_tensor(e_s[:, k % 2, :], e_s[:, k % 2, :], comb[slot][f][:, n * HALF:(n + 1) * HALF],
                                      ALU.mult).then_inc(e_comb, 1)

            run_experts(dve, experts)
            for n in range(NT // 2):
                dve.wait_ge(yb_ps, n + 1)
                xb = x_sb[:, 2 * n:2 * n + 2, :].rearrange("p a b -> p (a b)")
                dve.tensor_tensor(xb, xb, ps[:, n, :], ALU.add).then_inc(out_ready, 1)


_INS = ['x', 'itok_BxS_13_99985', 'ctx_2048', 'mask_1xSxS2_ff0', 'L0_ffn_w1', 'L0_ffn_w2', 'L1_xattn_Wq', 'L1_xattn_bq',
        'L1_xattn_Wk', 'L1_xattn_bk', 'L1_xattn_Wv', 'L1_xattn_bv', 'L1_xattn_Wo', 'L1_xattn_qn_w', 'L1_xattn_kn_w',
        'L1_ffn_gate_w', 'L1_ffn_wg', 'L1_ffn_wu', 'L1_ffn_wd', 'L1_ffn_sg', 'L1_ffn_su', 'L1_ffn_sd']
_OUTS = [((4, 256, 256), 'float32')]


def kernel(**inputs):
    import numpy as _np
    import concourse.bacc as _bacc
    from concourse import mybir as _mybir
    from concourse.bass_utils import run_bass_kernel_spmd as _run

    nc = _bacc.Bacc("TRN2", target_bir_lowering=False, num_devices=1)
    arrays, args = {}, []
    for name in _INS:
        a = _np.ascontiguousarray(inputs[name])
        arrays[f"in_{name}_dram"] = a
        args.append(nc.dram_tensor(f"in_{name}_dram", a.shape, _mybir.dt.from_np(a.dtype), kind="ExternalInput").ap())
    for i, (shape, dtype) in enumerate(_OUTS):
        dt = _mybir.dt.from_np(_np.dtype(dtype))
        args.append(nc.dram_tensor(f"out_{i}_dram", shape, dt, kind="ExternalOutput").ap())
    build_program(nc, *args)
    r = _run(nc, [arrays], core_ids=[0])
    return r.results[0]["out_0_dram"]
```
